# Optimizing a Trainium2 kernel written in Bass

```python
import numpy as np
import jax
import jax.numpy as jnp

def _softmax(x, axis=-1):
    return jax.nn.softmax(x, axis=axis)

def _gelu(x):
    return jax.nn.gelu(x, approximate=True)

def _silu(x):
    return jax.nn.silu(x)

def _sigmoid(x):
    return jax.nn.sigmoid(x)

def _layernorm(x, axis=-1, eps=1e-05):
    m = jnp.mean(x, axis=axis, keepdims=True)
    v = jnp.var(x, axis=axis, keepdims=True)
    return (x - m) / jnp.sqrt(v + eps)

def _scatter_add(tgt, idx, src, axis=0):
    return tgt.at[idx].add(src)

def _segment_sum(src, seg, n):
    return jax.ops.segment_sum(src, seg, n)
kernel_name = 'mk_flamingo_gated_d1_seqx_r4_92af99'

def setup_inputs(seed: int=0):
    np.random.seed(seed)
    _w = jnp.asarray

    def _rec_inputs():
        import jax
        import jax.numpy as jnp
        _rk = jax.random.key(seed)
        x = -0.000125 + 0.9999 * jax.random.normal(jax.random.fold_in(_rk, 1), (4, 512, 512), jnp.float32)
        _lenS = 512 - jax.random.randint(jax.random.fold_in(_rk, 7), (4,), 0, max(1, 512 // 4) + 1, jnp.int32)
        _lenS2 = 512 - jax.random.randint(jax.random.fold_in(_rk, 8), (4,), 0, max(1, 512 // 4) + 1, jnp.int32)
        _ctx_2048P = jax.random.normal(jax.random.fold_in(_rk, 11), (4, 16, 512), jnp.float32)
        _ctx_2048c = jax.random.dirichlet(jax.random.fold_in(_rk, 511), 0.3 * jnp.ones((16,), jnp.float32), (4, 512))
        _ctx_2048t = jnp.einsum('bsk,bkd->bsd', _ctx_2048c, _ctx_2048P)
        _ctx_2048t = _ctx_2048t * jax.lax.rsqrt(jnp.mean(jnp.square(_ctx_2048t)) + 1e-12) * 0.953939
        ctx_2048 = -1.52775e-05 + 0.999936 * (_ctx_2048t + 0.3 * jax.random.normal(jax.random.fold_in(_rk, 611), (4, 512, 512), jnp.float32))
        _g = jax.random.normal(jax.random.fold_in(_rk, 9001), (2, 1), jnp.float32)
        _g = jnp.sign(_g) * jnp.maximum(jnp.abs(_g), 1.0) + (_g == 0) * 1.0
        g_xattn = _g[0]
        g_ffn = _g[1]
        return (x, ctx_2048, g_xattn, g_ffn)
    x, ctx_2048, g_xattn, g_ffn = _rec_inputs()

    def _L0_xattn_setup():
        import jax, jax.numpy as jnp
        import numpy as np
        B, S, D, H = (4, 1024, 512, 16)
        HD = D // H
        key = jax.random.key(seed)
        ks = jax.random.split(key, 12)
        sc = 1.0 / np.sqrt(D)
        inp = {'q': jax.random.normal(ks[0], (B, S, D), jnp.float32), 'k': jax.random.normal(ks[1], (B, S, D), jnp.float32), 'v': jax.random.normal(ks[2], (B, S, D), jnp.float32), 'Wq': jax.random.normal(ks[3], (D, D), jnp.float32) * sc, 'bq': jnp.zeros((D,), jnp.float32), 'Wk': jax.random.normal(ks[4], (D, D), jnp.float32) * sc, 'bk': jnp.zeros((D,), jnp.float32), 'Wv': jax.random.normal(ks[5], (D, D), jnp.float32) * sc, 'bv': jnp.zeros((D,), jnp.float32), 'Wo': jax.random.normal(ks[6], (D, D), jnp.float32) * sc, 'bo': jnp.zeros((D,), jnp.float32)}
        return inp
    _L0_xattn_all = _L0_xattn_setup()
    _L0_xattn_in = {k: v for k, v in _L0_xattn_all.items() if k in ('Wq', 'bq', 'Wk', 'bk', 'Wv', 'bv', 'Wo', 'bo')}
    del _L0_xattn_all

    def _L0_ffn_setup():
        import jax, jax.numpy as jnp
        import numpy as np
        key = jax.random.key(seed)
        k1, k2, k3, k4 = jax.random.split(key, 4)
        B, S, D_IN, D_OUT = (4, 1024, 512, 512)
        x = jax.random.normal(k1, (B, S, D_IN), dtype=jnp.float32)
        weight = jax.random.normal(k2, (D_OUT, D_IN), dtype=jnp.float32) * 0.02
        scale_weight = jax.random.uniform(k3, (D_OUT,), dtype=jnp.float32, minval=0.5, maxval=1.5)
        bias = jax.random.normal(k4, (D_OUT,), dtype=jnp.float32) * 0.02
        return {'x': x, 'weight': weight, 'scale_weight': scale_weight, 'bias': bias}
    _L0_ffn_all = _L0_ffn_setup()
    _L0_ffn_in = {k: v for k, v in _L0_ffn_all.items() if k in ('weight', 'scale_weight', 'bias')}
    del _L0_ffn_all
    return {'x': x, 'ctx_2048': ctx_2048, 'g_xattn': g_xattn, 'g_ffn': g_ffn, 'L0_xattn_Wq': _L0_xattn_in['Wq'], 'L0_xattn_bq': _L0_xattn_in['bq'], 'L0_xattn_Wk': _L0_xattn_in['Wk'], 'L0_xattn_bk': _L0_xattn_in['bk'], 'L0_xattn_Wv': _L0_xattn_in['Wv'], 'L0_xattn_bv': _L0_xattn_in['bv'], 'L0_xattn_Wo': _L0_xattn_in['Wo'], 'L0_xattn_bo': _L0_xattn_in['bo'], 'L0_ffn_weight': _L0_ffn_in['weight'], 'L0_ffn_scale_weight': _L0_ffn_in['scale_weight'], 'L0_ffn_bias': _L0_ffn_in['bias']}

def reference(x, ctx_2048, g_xattn, g_ffn, L0_xattn_Wq, L0_xattn_bq, L0_xattn_Wk, L0_xattn_bk, L0_xattn_Wv, L0_xattn_bv, L0_xattn_Wo, L0_xattn_bo, L0_ffn_weight, L0_ffn_scale_weight, L0_ffn_bias):
    import jax
    import jax.numpy as jnp

    def _L0_xattn_ref(q, k, v, Wq, bq, Wk, bk, Wv, bv, Wo, bo):
        import jax, jax.numpy as jnp
        import numpy as np
        B, S, D, H = (4, 1024, 512, 16)
        HD = D // H
        bs, sl, nf = q.shape
        Q = (q @ Wq.T + bq).reshape(bs, sl, H, HD)
        K = (k @ Wk.T + bk).reshape(bs, sl, H, HD)
        V = (v @ Wv.T + bv).reshape(bs, sl, H, HD)
        score = jnp.einsum('bshd,bsgd->bshg', Q, K)
        weight = jax.nn.softmax(score, axis=-1)
        attn = jnp.einsum('bshg,bsgd->bshd', weight, V).reshape(bs, sl, nf)
        return attn @ Wo.T + bo

    def _L0_ffn_ref(x, weight, scale_weight, bias):
        import jax, jax.numpy as jnp
        import numpy as np
        w = weight * scale_weight[:, None]
        out = jnp.einsum('bsi,oi->bso', x, w) + bias
        return out
    x = x + jnp.tanh(g_xattn[0]) * _L0_xattn_ref(_layernorm(x, axis=-1), ctx_2048, ctx_2048, L0_xattn_Wq, L0_xattn_bq, L0_xattn_Wk, L0_xattn_bk, L0_xattn_Wv, L0_xattn_bv, L0_xattn_Wo, L0_xattn_bo)
    x = x + jnp.tanh(g_ffn[0]) * _L0_ffn_ref(_layernorm(x, axis=-1), L0_ffn_weight, L0_ffn_scale_weight, L0_ffn_bias)
    return x

_drawn_inputs = setup_inputs


def setup_inputs(seed=0):
    import zlib

    import numpy as np

    out = dict(_drawn_inputs(seed))
    spreads = {'L0_xattn_bq': (0.0, 0.1),
     'L0_xattn_bk': (0.0, 0.1),
     'L0_xattn_bv': (0.0, 0.1),
     'L0_xattn_bo': (0.0, 0.1)}
    factors = {'L0_ffn_bias': 4.096}
    for name, (base, spread) in spreads.items():
        noise = np.random.default_rng([zlib.crc32(name.encode()), seed]).standard_normal(out[name].shape)
        drawn = base * np.exp(spread * noise) if base else spread * noise
        out[name] = jnp.asarray(drawn.astype(out[name].dtype))
    for name, factor in factors.items():
        out[name] = (out[name] * factor).astype(out[name].dtype)
    return out
```

```python
from contextlib import ExitStack

import concourse.bass as bass
from concourse import mybir

F32 = mybir.dt.float32
F32R = mybir.dt.float32r
ALU = mybir.AluOpType
ACT = mybir.ActivationFunctionType
AXIS_X = mybir.AxisListType.X

P = 128
B, S, D = 4, 512, 512
H, HD = 16, 32
KC = D // P
QH = P // HD
TILES = 2
TOK = TILES * P
CHUNKS = B * S // TOK
PER_B = S // TOK
OCT = 8
OCTS = P // OCT
PAIRS = OCT // 2
HT = H * TILES
BANK = 512
OCTS_A_BANK = BANK // (2 * HT)
POOL_OCTS = 6
EPS = 1e-5
HI, LO = 0, 1
DMA = 16
MOVES = TILES * QH


def reached(engine, semaphore, value):
    if not (isinstance(value, int) and value <= 0):
        engine.wait_ge(semaphore, value)


def gated_attention_kernel(nc, x, ctx_t, g_attn, g_ffn, wq_t, bq, wk_t, bk, wv_t, bv, wo_t, bo,
                           wf_t, scale, bf, v_scratch, out):
    stack = ExitStack()
    with stack:
        def sb(name, shape, dt=F32):
            return stack.enter_context(nc.sbuf_tensor(name, shape, dt))

        def psum(name):
            return stack.enter_context(nc.psum_tensor(name, [P, BANK], F32))

        def sem(name):
            return stack.enter_context(nc.semaphore(name))

        weights = {n: sb(f"{n}_parts", [P, 2, KC, D], F32R) for n in ("wv", "wq", "wk", "wo", "wf")}
        ident = sb("ident", [P, P])
        same_token = sb("same_token", [P, OCT])
        bq_col, bk_col = sb("bq_col", [P, KC]), sb("bk_col", [P, KC])
        bv_row, bo_row, bf_row = sb("bv_row", [P, D]), sb("bo_row", [P, D]), sb("bf_row", [P, D])
        gates = sb("gates", [P, 2])
        tanh_g = sb("tanh_g", [P, 2])
        minus_half = sb("minus_half", [P, TILES])
        x_norm = sb("x_norm", [P, TILES, D])
        x_res = sb("x_res", [P, TILES, D])
        stats = [sb(f"stats{i}", [P, TILES, 6]) for i in (1, 2)]
        moments = [sb(f"moments{i}", [P, TILES, 2]) for i in (1, 2)]
        var_eps = [sb(f"var_eps{i}", [P, TILES]) for i in (1, 2)]
        rstd = [sb(f"rstd{i}", [P, TILES]) for i in (1, 2)]
        ctx_raw = sb("ctx_raw", [P, KC, TOK])
        ctx_parts = sb("ctx_parts", [P, 2, KC, TOK], F32R)
        xa_parts = sb("xa_parts", [P, 2, KC, TOK], F32R)
        x2_parts = sb("x2_parts", [P, 2, KC, TOK], F32R)
        q_t, k_t = sb("q_t", [P, KC, TOK]), sb("k_t", [P, KC, TOK])
        v_rows = sb("v_rows", [P, TILES, D])
        q_pad = sb("q_pad", [P, H, TILES, P])
        k_keys = sb("k_keys", [P, H, P])
        v_keys = sb("v_keys", [P, TILES * OCTS, HD])
        turned = sb("turned", [P, OCTS, 2, H, 2])
        peak = sb("peak", [P, OCTS, 2])
        probs = sb("probs", [P, OCTS, 2, H])
        total = sb("total", [P, OCTS, 2])
        inv_total = sb("inv_total", [P, OCTS, 2])
        probs_t = sb("probs_t", [P, OCTS, HT])
        spread = sb("spread", [P, OCTS, HT, OCT])
        w_raw = spread[:].rearrange("p o h t -> p (o h t)").rearrange("p (s k n) -> p s k n", s=2, k=KC)
        attn_cols = sb("attn_cols", [P // 2, H, P])
        attn_or_norm = sb("attn_or_norm", [P, KC * TOK])
        attn_t = attn_or_norm[:].rearrange("p (c n) -> p c n", c=KC)
        x2_norm = attn_or_norm[:].rearrange("p (t n) -> p t n", t=TILES)
        x2 = sb("x2", [P, TILES, D])

        acc = [psum(f"acc{i}") for i in range(2)]
        turn_ps = [psum(f"turn_ps{i}") for i in range(2)]
        score_ps = [psum(f"score_ps{i}") for i in range(2)]
        attn_ps = [psum(f"attn_ps{i}") for i in range(2)]

        consts_in = sem("consts_in")
        w_in = [sem(f"w_in{i}") for i in range(2)]
        x_in, res_in, ctx_in = sem("x_in"), sem("res_in"), sem("ctx_in")
        q_moved, k_moved = sem("q_moved"), sem("k_moved")
        a_moved = [sem(f"a_moved{t}") for t in range(TILES)]
        v_saved, v_in, y_saved = sem("v_saved"), sem("v_in"), sem("y_saved")
        sp_passed, dve_passed = sem("sp_passed"), sem("dve_passed")
        zeroed, consts_made, gates_done, rows_scaled = (
            sem("zeroed"), sem("consts_made"), sem("gates_done"), sem("rows_scaled"))
        w_scaled, w_hi, w_lo = sem("w_scaled"), sem("w_hi"), sem("w_lo")
        v_mm, q_mm, k_mm, o_mm, f_mm = (sem(n) for n in ("v_mm", "q_mm", "k_mm", "o_mm", "f_mm"))
        score_mm, attn_mm, x1_turned, x2_turned = (
            sem(n) for n in ("score_mm", "attn_mm", "x1_turned", "x2_turned"))
        v_out, q_out, k_out, o_out, f_out, a_out = (
            sem(n) for n in ("v_out", "q_out", "k_out", "o_out", "f_out", "a_out"))
        x1_hi, x1_lo, x2_hi, x2_lo, ctx_hi, ctx_lo, at_hi, at_lo = (
            sem(n) for n in ("x1_hi", "x1_lo", "x2_hi", "x2_lo", "ctx_hi", "ctx_lo", "at_hi", "at_lo"))
        s_turned, s_peak, s_sub, s_exp, s_total, s_inv, s_probs, s_back = (
            sem(n) for n in ("s_turned", "s_peak", "s_sub", "s_exp", "s_total", "s_inv", "s_probs", "s_back"))
        spread_dve, spread_pool = sem("spread_dve"), sem("spread_pool")
        n_stats = [sem(f"n{i}_stats") for i in (1, 2)]
        n_aggr = [sem(f"n{i}_aggr") for i in (1, 2)]
        n_eps = [sem(f"n{i}_eps") for i in (1, 2)]
        n_rstd = [sem(f"n{i}_rstd") for i in (1, 2)]
        n_done = [sem(f"n{i}_done") for i in (1, 2)]
        res_biased, x2_biased = sem("res_biased"), sem("x2_biased")

        x_rows = x.rearrange("b s d -> (b s) d")
        out_rows = out.rearrange("b s d -> (b s) d")

        def tiles_of(rows, c):
            return rows[bass.ds(c * TOK, TOK), :].rearrange("(t p) n -> p t n", p=P)

        def pieces(w):
            return w.rearrange("(k p) n -> p k n", p=P)

        W_ORDER = [("wv", wv_t), ("wq", wq_t), ("wk", wk_t), ("wo", wo_t), ("wf", wf_t)]

        block = stack.enter_context(nc.Block())

        def steps(engine, step):
            step(0, before=False, after=True, after2=True)
            with engine.Fori(1, CHUNKS - 2) as i:
                step(i, before=True, after=True, after2=True)
            step(CHUNKS - 2, before=True, after=True, after2=False)
            step(CHUNKS - 1, before=True, after=False, after2=False)

        @block.sync
        def _(sp):
            def load_x(c):
                reached(sp, x1_turned, TILES * c)
                sp.sem_inc(sp_passed, 1)
                sp.dma_start(x_norm[:], tiles_of(x_rows, c)).then_inc(x_in, DMA)

            def load_res(c):
                reached(sp, o_out, TILES * c)
                sp.sem_inc(sp_passed, 1)
                sp.dma_start(x_res[:], tiles_of(x_rows, c)).then_inc(res_in, DMA)

            def load_ctx(c):
                reached(sp, ctx_lo, c)
                sp.sem_inc(sp_passed, 1)
                sp.dma_start(ctx_raw[:], ctx_t[:, bass.ds(c * TOK, TOK)].rearrange(
                    "(k p) n -> p k n", p=P)).then_inc(ctx_in, DMA)

            def move_q(c):
                sp.wait_ge(q_out, KC * (c + 1))
                sp.sem_inc(sp_passed, 1)
                reached(sp, score_mm, 2 * c)
                for t in range(TILES):
                    for q in range(QH):
                        sp.dma_start(
                            q_pad[HD * t:HD * (t + 1), q::QH, t, :],
                            q_t[HD * q:HD * (q + 1), :, P * t:P * (t + 1)]).then_inc(q_moved, DMA)

            def move_k(c):
                sp.wait_ge(k_out, KC * (c + 1))
                sp.sem_inc(sp_passed, 1)
                reached(sp, score_mm, 2 * c)
                for t in range(TILES):
                    for q in range(QH):
                        sp.dma_start(
                            k_keys[HD * t:HD * (t + 1), q::QH, :],
                            k_t[HD * q:HD * (q + 1), :, P * t:P * (t + 1)]).then_inc(k_moved, DMA)

            def save_v(c):
                sp.wait_ge(v_out, TILES * (c + 1))
                sp.sem_inc(sp_passed, 1)
                for t in range(TILES):
                    sp.dma_start(v_scratch[bass.ds(c * TOK + P * t, P), :].rearrange("(n s) e -> s n e", s=2),
                                 v_rows[:, t, :]).then_inc(v_saved, DMA)

            def load_v(c):
                sp.wait_ge(v_saved, TILES * DMA * (c + 1))
                reached(sp, attn_mm, 2 * c)
                sp.sem_inc(sp_passed, 1)
                sp.dma_start(v_keys[:], v_scratch[bass.ds(c * TOK, TOK), :].rearrange(
                    "(o t) (g d) -> (t g) o d", t=OCT, d=HD)).then_inc(v_in, DMA)

            def move_attn(c):
                sp.wait_ge(a_out, 4 * (c + 1))
                sp.sem_inc(sp_passed, 1)
                reached(sp, x2_turned, TILES * c)
                for t in range(TILES):
                    for q in range(QH):
                        sp.dma_start(
                            attn_t[HD * q:HD * (q + 1), :, P * t:P * (t + 1)],
                            attn_cols[HD * t:HD * (t + 1), q::QH, :]).then_inc(a_moved[t], DMA)

            def save_y(c):
                sp.wait_ge(f_out, TILES * (c + 1))
                sp.sem_inc(sp_passed, 1)
                sp.dma_start(tiles_of(out_rows, c), x2[:]).then_inc(y_saved, DMA)

            load_x(0)
            load_ctx(0)
            for n, (_, w) in enumerate(W_ORDER):
                if n >= 2:
                    sp.wait_ge(w_lo, n - 1)
                sp.dma_start(w_raw[:, n % 2], pieces(w)).then_inc(w_in[n % 2], DMA)
                if n == 1:
                    for col, dram in ((bq_col, bq), (bk_col, bk)):
                        sp.dma_start(col[:], dram).then_inc(consts_in, DMA)
                    for row, dram in ((bv_row, bv), (bo_row, bo), (bf_row, bf)):
                        sp.dma_start(row[:], dram.partition_broadcast(P)).then_inc(consts_in, DMA)
                    for n_gate, dram in enumerate((g_attn, g_ffn)):
                        sp.dma_start(gates[:, n_gate:n_gate + 1],
                                     dram.partition_broadcast(P)).then_inc(consts_in, DMA)
                    sp.dma_start(x2[:, 0, :], scale.partition_broadcast(P)).then_inc(consts_in, DMA)
                    load_x(1)
                    load_ctx(1)
            sp.wait_ge(zeroed, 2)
            save_v(0)
            move_q(0)
            load_v(0)
            move_k(0)
            load_x(2)

            def step(i, before, after, after2):
                load_res(i)
                if after2:
                    load_ctx(i + 2)
                if after:
                    save_v(i + 1)
                    move_q(i + 1)
                move_attn(i)
                if after:
                    load_v(i + 1)
                    move_k(i + 1)
                if before:
                    save_y(i - 1)

            def step_and_x(i, before, after, after2):
                step(i, before, after, after2)
                if after2:
                    load_next_x(i)

            def load_next_x(i):
                if isinstance(i, int):
                    if i + 3 < CHUNKS:
                        load_x(i + 3)
                else:
                    load_x(i + 3)

            step_and_x(0, False, True, True)
            with sp.Fori(1, CHUNKS - 3) as i:
                step_and_x(i, True, True, True)
            step_and_x(CHUNKS - 3, True, True, True)
            step(CHUNKS - 2, True, True, False)
            step(CHUNKS - 1, True, False, False)
            save_y(CHUNKS - 1)
            sp.wait_ge(v_saved, TILES * DMA * CHUNKS)
            sp.wait_ge(y_saved, DMA * CHUNKS)

        @block.tensor
        def _(pe):
            def bank_free(user, c, b):
                if user in ("v", "o", "f"):
                    pe.wait_ge({"v": v_out, "o": o_out, "f": f_out}[user], TILES * c + b + 1)
                elif user:
                    pe.wait_ge({"q": q_out, "k": k_out}[user], KC * c + 2 * (b + 1))

            def product(dst, left, right):
                terms = [(k, a, b) for k in range(KC) for a, b in ((HI, HI), (HI, LO), (LO, HI))]
                for n, (k, a, b) in enumerate(terms):
                    last = pe.matmul(dst, left(a, k), right(b, k), start=(n == 0), stop=(n == len(terms) - 1))
                return last

            def rows_layer(parts, w, done, ready=None):
                for t in range(TILES):
                    if ready:
                        ready(t)
                    product(acc[t][:], lambda a, k: parts[:, a, k, P * t:P * (t + 1)],
                            lambda b, k: weights[w][:, b, k, :]).then_inc(done, 1)

            def cols_layer(w, parts, done, prev, prev_c):
                for b in range(2):
                    bank_free(prev, prev_c, b)
                    for m in (2 * b, 2 * b + 1):
                        last = product(acc[b][:, TOK * (m % 2):TOK * (m % 2 + 1)],
                                       lambda a, k: weights[w][:, a, k, P * m:P * (m + 1)],
                                       lambda c, k: parts[:, c, k, :])
                    last.then_inc(done, 1)

            def turn(src, done, t):
                for k in range(KC):
                    last = pe.transpose(turn_ps[t][:, P * k:P * (k + 1)], src[:, t, P * k:P * (k + 1)], ident[:])
                last.then_inc(done, 1)

            def turn_x1(c, prev):
                for t in range(TILES):
                    pe.wait_ge(n_done[0], TILES * c + t + 1)
                    prev(t)
                    turn(x_norm, x1_turned, t)

            def turn_x2(c, prev):
                for t in range(TILES):
                    pe.wait_ge(n_done[1], TILES * c + t + 1)
                    prev(t)
                    turn(x2_norm, x2_turned, t)

            def x1_read(c):
                return lambda t: pe.wait_ge(x1_lo, TILES * c + t + 1)

            def x2_read(c):
                return lambda t: pe.wait_ge(x2_lo, TILES * c + t + 1)

            def v_layer(c, prev, prev_c):
                pe.wait_ge(ctx_lo, c + 1)
                rows_layer(ctx_parts, "wv", v_mm, lambda t: bank_free(prev, prev_c, t))

            def q_layer(c):
                pe.wait_ge(x1_lo, TILES * (c + 1))
                cols_layer("wq", xa_parts, q_mm, "v", c)

            def k_layer(c):
                cols_layer("wk", ctx_parts, k_mm, "q", c)

            def o_layer(c, prev, prev_c):
                def ready(t):
                    pe.wait_ge(at_lo, TILES * c + t + 1)
                    bank_free(prev, prev_c, t)
                rows_layer(xa_parts, "wo", o_mm, ready)

            def f_layer(c, prev, prev_c):
                def ready(t):
                    pe.wait_ge(x2_lo, TILES * c + t + 1)
                    bank_free(prev, prev_c, t)
                rows_layer(x2_parts, "wf", f_mm, ready)

            def score(c):
                pe.wait_ge(q_moved, DMA * MOVES * (c + 1))
                pe.wait_ge(k_moved, DMA * MOVES * (c + 1))
                for b in range(2):
                    reached(pe, s_turned, 2 * c if isinstance(c, int) and c == 0 else 2 * c - 1 + b)
                    for o in range(OCTS_A_BANK):
                        for pair in range(PAIRS):
                            n = PAIRS * (OCTS_A_BANK * b + o) + pair
                            last = pe.matmul(
                                score_ps[b][HD * pair:HD * (pair + 1), 2 * HT * o:2 * HT * (o + 1)],
                                k_keys[:].rearrange("p g (s n) -> p (g s) n", s=2)[:, :, n],
                                q_pad[:].rearrange("p h t (s n) -> p s (h t) n", s=2)[:, :, :, n],
                                start=True, stop=True)
                    last.then_inc(score_mm, 1)

            def attend(c):
                pe.wait_ge(v_in, DMA * (c + 1))
                pe.wait_ge(spread_dve, c + 1)
                pe.wait_ge(spread_pool, c + 1)
                half = OCTS // 2
                for b in range(2):
                    reached(pe, a_out, 4 * c)
                    for o in range(half // 2):
                        for hf in range(2):
                            for t in range(TILES):
                                octet = half * hf + half // 2 * b + o
                                tile = TILES * hf + t
                                last = pe.matmul(
                                    attn_ps[b][HD * tile:HD * (tile + 1), P * o:P * (o + 1)],
                                    v_keys[:, OCTS * t + octet, :],
                                    spread[:, octet, t::TILES, :], start=True, stop=True)
                    last.then_inc(attn_mm, 1)

            pe.wait_ge(consts_made, 1)
            turn_x1(0, lambda t: None)
            pe.wait_ge(w_lo, 1)
            v_layer(0, None, 0)
            pe.wait_ge(w_lo, 2)
            q_layer(0)
            pe.wait_ge(w_lo, 3)
            k_layer(0)
            turn_x1(1, x1_read(0))
            pe.wait_ge(w_lo, 5)

            def tensor_step(i, before, after, after2):
                score(i)
                if before:
                    turn_x2(i - 1, x1_read(i + 1) if after else x2_read(i - 2))
                if after:
                    v_layer(i + 1, *(("o", i - 1) if before else ("k", 0)))
                    q_layer(i + 1)
                attend(i)
                if after:
                    k_layer(i + 1)
                if before:
                    f_layer(i - 1, *(("k", i + 1) if after else ("o", i - 1)))
                o_layer(i, *(("f", i - 1) if before else ("k", 1)))
                if after2:
                    turn_x1(i + 2, x2_read(i - 1) if before else x1_read(1))

            steps(pe, tensor_step)
            last = CHUNKS - 1
            turn_x2(last, x2_read(last - 1))
            f_layer(last, "o", last)

        @block.scalar
        def _(act):
            def high(dst, src):
                return nc.scalar.activation(dst, src, ACT.Identity)

            def turned_hi(parts, ready, done, c, free):
                for t in range(TILES):
                    act.wait_ge(ready, TILES * c + t + 1)
                    free()
                    high(parts[:, HI, :, P * t:P * (t + 1)],
                         turn_ps[t][:].rearrange("p (k n) -> p k n", k=KC)).then_inc(done, 1)

            def x1_high(c):
                turned_hi(xa_parts, x1_turned, x1_hi, c, lambda: (
                    reached(act, o_mm, TILES * (c - 1)), reached(act, q_mm, 2 * c)))

            def x2_high(c):
                turned_hi(x2_parts, x2_turned, x2_hi, c, lambda: reached(act, f_mm, TILES * c))

            def ctx_high(c):
                act.wait_ge(ctx_in, DMA * (c + 1))
                reached(act, k_mm, 2 * c)
                high(ctx_parts[:, HI], ctx_raw[:]).then_inc(ctx_hi, 1)

            def exp(c):
                act.wait_ge(s_sub, c + 1)
                nc.scalar.activation(probs[:], probs[:], ACT.Exp).then_inc(s_exp, 1)

            def q_bias(c):
                reached(act, q_moved, DMA * MOVES * c)
                for m in range(KC):
                    if m % 2 == 0:
                        act.wait_ge(q_mm, 2 * c + m // 2 + 1)
                    nc.scalar.activation(q_t[:, m, :], acc[m // 2][:, TOK * (m % 2):TOK * (m % 2 + 1)],
                                         ACT.Identity, bias=bq_col[:, m:m + 1]).then_inc(q_out, 1)

            def attn_copy(c):
                for t in range(TILES):
                    reached(act, a_moved[t], DMA * QH * c)
                for b in range(2):
                    act.wait_ge(attn_mm, 2 * c + b + 1)
                    for hf in range(2):
                        n = P // 4 * hf + P // 8 * b
                        nc.scalar.activation(
                            attn_cols[:].rearrange("p h (s n) -> p (h s) n", s=2)[:, :, n:n + P // 8]
                            .rearrange("p e (o n) -> p o e n", n=PAIRS),
                            attn_ps[b][P // 2 * hf:P // 2 * (hf + 1), :].rearrange(
                                "p (o e n) -> p o e n", e=2 * H, n=PAIRS), ACT.Identity).then_inc(a_out, 1)

            def attn_high(c):
                reached(act, q_mm, 2 * (c + 2) if not (isinstance(c, int) and c == CHUNKS - 1) else 2 * CHUNKS)
                for t in range(TILES):
                    act.wait_ge(a_moved[t], DMA * QH * (c + 1))
                    high(xa_parts[:, HI, :, P * t:P * (t + 1)],
                         attn_t[:, :, P * t:P * (t + 1)]).then_inc(at_hi, 1)

            def w_high(n):
                name = W_ORDER[n][0]
                if name == "wf":
                    act.wait_ge(w_scaled, 1)
                else:
                    act.wait_ge(w_in[n % 2], DMA * (n // 2 + 1))
                high(weights[name][:, HI], w_raw[:, n % 2]).then_inc(w_hi, 1)

            w_high(0)
            ctx_high(0)
            x1_high(0)
            w_high(1)
            w_high(2)
            act.wait_ge(consts_in, 8 * DMA)
            nc.scalar.activation(tanh_g[:], gates[:], ACT.Tanh).then_inc(gates_done, 1)
            q_bias(0)
            w_high(3)
            w_high(4)
            ctx_high(1)
            x1_high(1)

            def scalar_step(i, before, after, after2):
                if before:
                    x2_high(i - 1)
                exp(i)
                if after:
                    q_bias(i + 1)
                attn_copy(i)
                if after2:
                    ctx_high(i + 2)
                attn_high(i)
                if after2:
                    x1_high(i + 2)

            steps(act, scalar_step)
            x2_high(CHUNKS - 1)

        @block.vector
        def _(dve):
            def low(dst, src, hi):
                return nc.vector.tensor_tensor(dst, src, hi.bitcast(F32), ALU.subtract)

            def turned_lo(parts, hi_done, done, c):
                for t in range(TILES):
                    dve.wait_ge(hi_done, TILES * c + t + 1)
                    n = slice(P * t, P * (t + 1))
                    low(parts[:, LO, :, n], turn_ps[t][:].rearrange("p (k n) -> p k n", k=KC),
                        parts[:, HI, :, n]).then_inc(done, 1)

            def norm_stats(which, src, c):
                for t in range(TILES):
                    if which == 0 and t == 0:
                        dve.wait_ge(x_in, DMA * (c + 1))
                    if which == 1:
                        dve.wait_ge(o_out, TILES * c + t + 1)
                    nc.vector.bn_stats(stats[which][:, t, :], src[:, t, :]).then_inc(n_stats[which], 1)
                dve.wait_ge(n_stats[which], TILES * (c + 1))
                dve.sem_inc(dve_passed, 1)
                for t in range(TILES):
                    nc.vector.bn_aggr(moments[which][:, t, :], stats[which][:, t, :]).then_inc(n_aggr[which], 1)
                dve.wait_ge(n_aggr[which], TILES * (c + 1))
                nc.vector.tensor_scalar(var_eps[which][:], moments[which][:, :, 1], EPS, None,
                                        ALU.add).then_inc(n_eps[which], 1)

            def norm_apply(which, src, dst, c):
                dve.wait_ge(n_rstd[which], c + 1)
                for t in range(TILES):
                    nc.vector.tensor_scalar(dst[:, t, :], src[:, t, :], moments[which][:, t, 0:1],
                                            rstd[which][:, t:t + 1], ALU.subtract, ALU.mult
                                            ).then_inc(n_done[which], 1)

            def w_low(n):
                name = W_ORDER[n][0]
                dve.wait_ge(w_hi, n + 1)
                low(weights[name][:, LO], w_raw[:, n % 2], weights[name][:, HI]).then_inc(w_lo, 1)

            def v_bias(c):
                def tile(t):
                    dve.wait_ge(v_mm, TILES * c + t + 1)
                    reached(dve, v_saved, TILES * DMA * c)
                    nc.vector.tensor_tensor(v_rows[:, t, :], acc[t][:], bv_row[:], ALU.add).then_inc(v_out, 1)
                return tile

            def k_bias(c):
                reached(dve, k_moved, DMA * MOVES * c)
                for m in range(KC):
                    if m % 2 == 0:
                        dve.wait_ge(k_mm, 2 * c + m // 2 + 1)
                    nc.vector.tensor_scalar(k_t[:, m, :], acc[m // 2][:, TOK * (m % 2):TOK * (m % 2 + 1)],
                                            bk_col[:, m:m + 1], None, ALU.add).then_inc(k_out, 1)

            def scores_turn(c):
                flat = turned[:].rearrange("p o a g b -> p (o a g b)")
                for b in range(2):
                    dve.wait_ge(score_mm, 2 * c + b + 1)
                    nc.vector.transpose(flat[:, BANK * b:BANK * (b + 1)], score_ps[b][:]).then_inc(s_turned, 1)

            def own(token):
                return turned[:, :, token, :, token]

            def softmax_a(c):
                dve.wait_ge(s_turned, 2 * (c + 1))
                for s in range(2):
                    nc.vector.tensor_reduce(peak[:, :, s], own(s), AXIS_X, ALU.max).then_inc(s_peak, 1)
                for s in range(2):
                    dve.wait_ge(s_peak, 2 * c + s + 1)
                    last = nc.vector.tensor_tensor(probs[:, :, s, :], own(s),
                                                   peak[:, :, s].unsqueeze(2).broadcast_to([P, OCTS, H]),
                                                   ALU.subtract)
                last.then_inc(s_sub, 1)

            def softmax_b(c):
                dve.wait_ge(s_exp, c + 1)
                nc.vector.tensor_reduce(total[:], probs[:], AXIS_X, ALU.add).then_inc(s_total, 1)
                dve.wait_ge(s_total, c + 1)
                nc.vector.reciprocal(inv_total[:], total[:]).then_inc(s_inv, 1)
                dve.wait_ge(s_inv, c + 1)
                nc.vector.tensor_tensor(probs[:], probs[:], inv_total[:].unsqueeze(3).broadcast_to([P, OCTS, 2, H]),
                                        ALU.mult).then_inc(s_probs, 1)
                dve.wait_ge(s_probs, c + 1)
                nc.vector.transpose(probs_t[:].rearrange("p o c -> p (o c)"),
                                    probs[:].rearrange("p o s g -> p (o s g)")).then_inc(s_back, 1)

            def spread_part(c, first, last_octet):
                n = last_octet - first
                return nc.vector.tensor_tensor(
                    spread[:, first:last_octet].rearrange("p o h t -> p (o h) t"),
                    probs_t[:, first:last_octet].rearrange("p o h -> p (o h)").unsqueeze(2).broadcast_to(
                        [P, n * HT, OCT]),
                    same_token[:].unsqueeze(1).broadcast_to([P, n * HT, OCT]), ALU.mult)

            def attn_low(c):
                for t in range(TILES):
                    dve.wait_ge(at_hi, TILES * c + t + 1)
                    n = slice(P * t, P * (t + 1))
                    low(xa_parts[:, LO, :, n], attn_t[:, :, n], xa_parts[:, HI, :, n]).then_inc(at_lo, 1)

            def f_residual(c):
                for t in range(TILES):
                    dve.wait_ge(f_mm, TILES * c + t + 1)
                    dve.wait_ge(x2_biased, TILES * c + t + 1)
                    nc.vector.scalar_tensor_tensor(x2[:, t, :], acc[t][:], tanh_g[:, 1:2], x2[:, t, :],
                                                   ALU.mult, ALU.add).then_inc(f_out, 1)

            def o_residual(c):
                reached(dve, y_saved, DMA * c)
                for t in range(TILES):
                    dve.wait_ge(o_mm, TILES * c + t + 1)
                    dve.wait_ge(res_biased, TILES * c + t + 1)
                    nc.vector.scalar_tensor_tensor(x2[:, t, :], acc[t][:], tanh_g[:, 0:1], x_res[:, t, :],
                                                   ALU.mult, ALU.add).then_inc(o_out, 1)

            nc.vector.memset(q_pad[:], 0.0).then_inc(zeroed, 1)
            norm_stats(0, x_norm, 0)
            nc.vector.memset(k_keys[:], 0.0).then_inc(zeroed, 1)
            norm_apply(0, x_norm, x_norm, 0)
            w_low(0)
            turned_lo(xa_parts, x1_hi, x1_lo, 0)
            w_low(1)
            dve.wait_ge(consts_in, 8 * DMA)
            first_v = v_bias(0)
            first_v(0)
            first_v(1)
            w_low(2)
            norm_stats(0, x_norm, 1)
            norm_apply(0, x_norm, x_norm, 1)
            dve.wait_ge(w_in[0], 3 * DMA)
            nc.vector.tensor_tensor(w_raw[:, 0], w_raw[:, 0], x2[:, 0, :].unsqueeze(1).broadcast_to([P, KC, D]),
                                    ALU.mult).then_inc(w_scaled, 1)
            dve.wait_ge(gates_done, 1)
            for row, n in ((bo_row, 0), (bf_row, 1)):
                nc.vector.tensor_scalar(row[:], row[:], tanh_g[:, n:n + 1], None, ALU.mult).then_inc(rows_scaled, 1)
            k_bias(0)
            w_low(3)
            w_low(4)
            turned_lo(xa_parts, x1_hi, x1_lo, 1)

            def vector_step(i, before, after, after2):
                scores_turn(i)
                softmax_a(i)
                if before:
                    turned_lo(x2_parts, x2_hi, x2_lo, i - 1)
                softmax_b(i)
                v_tile = v_bias(i + 1) if after else (lambda t: None)
                v_tile(0)
                dve.wait_ge(s_back, i + 1)
                reached(dve, attn_mm, 2 * i)
                mid = (OCTS - POOL_OCTS) // 2
                spread_part(i, 0, mid)
                v_tile(1)
                spread_part(i, mid, OCTS - POOL_OCTS).then_inc(spread_dve, 1)
                if after2:
                    norm_stats(0, x_norm, i + 2)
                    norm_apply(0, x_norm, x_norm, i + 2)
                if after:
                    k_bias(i + 1)
                if before:
                    f_residual(i - 1)
                attn_low(i)
                o_residual(i)
                norm_stats(1, x2, i)
                norm_apply(1, x2, x2_norm, i)
                if after2:
                    turned_lo(xa_parts, x1_hi, x1_lo, i + 2)

            steps(dve, vector_step)
            turned_lo(x2_parts, x2_hi, x2_lo, CHUNKS - 1)
            f_residual(CHUNKS - 1)

        @block.gpsimd
        def _(pool):
            def root(which, c):
                pool.wait_ge(n_eps[which], c + 1)
                nc.gpsimd.tensor_tensor(rstd[which][:], var_eps[which][:], minus_half[:],
                                        ALU.pow).then_inc(n_rstd[which], 1)

            def ctx_low(c):
                pool.wait_ge(ctx_hi, c + 1)
                nc.gpsimd.tensor_tensor(ctx_parts[:, LO], ctx_raw[:], ctx_parts[:, HI].bitcast(F32),
                                        ALU.subtract).then_inc(ctx_lo, 1)

            def res_bias(c):
                pool.wait_ge(res_in, DMA * (c + 1))
                for t in range(TILES):
                    nc.gpsimd.tensor_tensor(x_res[:, t, :], x_res[:, t, :], bo_row[:], ALU.add
                                            ).then_inc(res_biased, 1)

            def x2_bias(c):
                for t in range(TILES):
                    pool.wait_ge(n_done[1], TILES * c + t + 1)
                    nc.gpsimd.tensor_tensor(x2[:, t, :], x2[:, t, :], bf_row[:], ALU.add
                                            ).then_inc(x2_biased, 1)

            def spread_last(c):
                pool.wait_ge(s_back, c + 1)
                reached(pool, attn_mm, 2 * c)
                first = OCTS - POOL_OCTS
                nc.gpsimd.tensor_tensor(
                    spread[:, first:].rearrange("p o h t -> p (o h) t"),
                    probs_t[:, first:].rearrange("p o h -> p (o h)").unsqueeze(2).broadcast_to(
                        [P, POOL_OCTS * HT, OCT]),
                    same_token[:].unsqueeze(1).broadcast_to([P, POOL_OCTS * HT, OCT]),
                    ALU.mult).then_inc(spread_pool, 1)

            made = sem("made")
            nc.gpsimd.memset(ident[:], 0.0).then_inc(made, 1)
            nc.gpsimd.memset(same_token[:], 1.0).then_inc(made, 1)
            nc.gpsimd.memset(minus_half[:], -0.5).then_inc(made, 1)
            pool.wait_ge(made, 3)
            nc.gpsimd.affine_select(out=ident[:], in_=ident[:], compare_op=ALU.not_equal, fill=1.0, base=0,
                                    pattern=[[-1, P]], channel_multiplier=1).then_inc(consts_made, 1)
            root(0, 0)
            nc.gpsimd.affine_select(out=same_token[:], in_=same_token[:], compare_op=ALU.is_ge, fill=0.0, base=0,
                                    pattern=[[-H, 2], [-2 * H, PAIRS]], channel_multiplier=1).then_inc(made, 1)
            pool.wait_ge(made, 4)
            nc.gpsimd.affine_select(out=same_token[:], in_=same_token[:], compare_op=ALU.is_ge, fill=0.0,
                                    base=H - 1, pattern=[[H, 2], [2 * H, PAIRS]], channel_multiplier=-1).then_inc(consts_made, 1)
            ctx_low(0)
            root(0, 1)
            ctx_low(1)
            pool.wait_ge(rows_scaled, 2)
            pool.wait_ge(w_lo, 5)
            pool.wait_ge(consts_made, 2)

            def pool_step(i, before, after, after2):
                spread_last(i)
                if after2:
                    root(0, i + 2)
                res_bias(i)
                if after2:
                    ctx_low(i + 2)
                root(1, i)
                x2_bias(i)

            steps(pool, pool_step)


def kernel(**inputs):
    import numpy as _np
    import concourse.bacc as _bacc
    from concourse import mybir as _mybir
    from concourse.bass_utils import run_bass_kernel_spmd as _run

    a = {k: _np.asarray(v) for k, v in inputs.items()}

    def cols(v):
        return v.reshape(KC, P).T

    arrays = {
        "x": a["x"],
        "ctx_t": a["ctx_2048"].reshape(B * S, D).T,
        "g_attn": a["g_xattn"],
        "g_ffn": a["g_ffn"],
        "wq_t": a["L0_xattn_Wq"].T, "bq": cols(a["L0_xattn_bq"]),
        "wk_t": a["L0_xattn_Wk"].T, "bk": cols(a["L0_xattn_bk"]),
        "wv_t": a["L0_xattn_Wv"].T, "bv": a["L0_xattn_bv"],
        "wo_t": a["L0_xattn_Wo"].T, "bo": a["L0_xattn_bo"],
        "wf_t": a["L0_ffn_weight"].T, "scale": a["L0_ffn_scale_weight"], "bf": a["L0_ffn_bias"],
    }
    arrays = {k: _np.ascontiguousarray(v) for k, v in arrays.items()}
    nc = _bacc.Bacc("TRN2", target_bir_lowering=False, num_devices=1)
    args = [nc.dram_tensor(k, v.shape, _mybir.dt.from_np(v.dtype), kind="ExternalInput").ap()
            for k, v in arrays.items()]
    args.append(nc.dram_tensor("v_scratch", (B * S, D), _mybir.dt.float32, kind="Internal").ap())
    args.append(nc.dram_tensor("out", (B, S, D), _mybir.dt.float32, kind="ExternalOutput").ap())
    gated_attention_kernel(nc, *args)
    r = _run(nc, [arrays], core_ids=[0])
    return r.results[0]["out"]
```

```python
from contextlib import ExitStack

import concourse.bass as bass
from concourse import mybir

F32 = mybir.dt.float32
F32R = mybir.dt.float32r
ALU = mybir.AluOpType
ACT = mybir.ActivationFunctionType
AXIS_X = mybir.AxisListType.X

P = 128
B, S, D = 4, 512, 512
H, HD = 16, 32
KC = D // P
QH = P // HD
TILES = 2
TOK = TILES * P
CHUNKS = B * S // TOK
PER_B = S // TOK
OCT = 8
OCTS = P // OCT
PAIRS = OCT // 2
HT = H * TILES
BANK = 512
OCTS_A_BANK = BANK // (2 * HT)
POOL_OCTS = 6
EPS = 1e-5
HI, LO = 0, 1
DMA = 16
MOVES = TILES * QH


def reached(engine, semaphore, value):
    if not (isinstance(value, int) and value <= 0):
        engine.wait_ge(semaphore, value)


def gated_attention_kernel(nc, x, ctx_t, g_attn, g_ffn, wq_t, bq, wk_t, bk, wv_t, bv, wo_t, bo,
                           wf_t, scale, bf, v_scratch, out):
    stack = ExitStack()
    with stack:
        def sb(name, shape, dt=F32):
            return stack.enter_context(nc.sbuf_tensor(name, shape, dt))

        def psum(name):
            return stack.enter_context(nc.psum_tensor(name, [P, BANK], F32))

        def sem(name):
            return stack.enter_context(nc.semaphore(name))

        weights = {n: sb(f"{n}_parts", [P, 2, KC, D], F32R) for n in ("wv", "wq", "wk", "wo", "wf")}
        ident = sb("ident", [P, P])
        same_token = sb("same_token", [P, OCT])
        bq_col, bk_col = sb("bq_col", [P, KC]), sb("bk_col", [P, KC])
        bv_row, bo_row, bf_row = sb("bv_row", [P, D]), sb("bo_row", [P, D]), sb("bf_row", [P, D])
        gates = sb("gates", [P, 2])
        tanh_g = sb("tanh_g", [P, 2])
        minus_half = sb("minus_half", [P, TILES])
        x_norm = sb("x_norm", [P, TILES, D])
        x_res = sb("x_res", [P, TILES, D])
        stats = [sb(f"stats{i}", [P, TILES, 6]) for i in (1, 2)]
        moments = [sb(f"moments{i}", [P, TILES, 2]) for i in (1, 2)]
        var_eps = [sb(f"var_eps{i}", [P, TILES]) for i in (1, 2)]
        rstd = [sb(f"rstd{i}", [P, TILES]) for i in (1, 2)]
        ctx_raw = sb("ctx_raw", [P, KC, TOK])
        ctx_parts = sb("ctx_parts", [P, 2, KC, TOK], F32R)
        xa_parts = sb("xa_parts", [P, 2, KC, TOK], F32R)
        x2_parts = sb("x2_parts", [P, 2, KC, TOK], F32R)
        q_t, k_t = sb("q_t", [P, KC, TOK]), sb("k_t", [P, KC, TOK])
        v_or_norm = sb("v_or_norm", [P, TILES, D])
        v_rows = x2_norm = v_or_norm
        q_pad = sb("q_pad", [P, H, TILES, P])
        k_keys = sb("k_keys", [P, H, P])
        v_keys = sb("v_keys", [P, TILES * OCTS, HD])
        turned = sb("turned", [P, OCTS, 2, H, 2])
        peak = sb("peak", [P, OCTS, 2])
        probs = sb("probs", [P, OCTS, 2, H])
        total = sb("total", [P, OCTS, 2])
        inv_total = sb("inv_total", [P, OCTS, 2])
        probs_t = sb("probs_t", [P, OCTS, HT])
        spread = sb("spread", [P, OCTS, HT, OCT])
        w_raw = spread[:].rearrange("p o h t -> p (o h t)").rearrange("p (s k n) -> p s k n", s=2, k=KC)
        attn_cols = sb("attn_cols", [P // 2, H, P])
        attn_t = sb("attn_t", [P, KC, TOK])
        x2 = sb("x2", [P, TILES, D])

        acc = [psum(f"acc{i}") for i in range(2)]
        turn_ps = [psum(f"turn_ps{i}") for i in range(2)]
        score_ps = [psum(f"score_ps{i}") for i in range(2)]
        attn_ps = [psum(f"attn_ps{i}") for i in range(2)]

        consts_in = sem("consts_in")
        w_in = [sem(f"w_in{i}") for i in range(2)]
        x_in, res_in, ctx_in = sem("x_in"), sem("res_in"), sem("ctx_in")
        q_moved, k_moved = sem("q_moved"), sem("k_moved")
        a_moved = [sem(f"a_moved{t}") for t in range(TILES)]
        v_saved, v_in = sem("v_saved"), sem("v_in")
        y_saved = [sem(f"y_saved{t}") for t in range(TILES)]
        sp_passed, dve_passed = sem("sp_passed"), sem("dve_passed")
        zeroed, consts_made, gates_done, rows_scaled = (
            sem("zeroed"), sem("consts_made"), sem("gates_done"), sem("rows_scaled"))
        w_scaled, w_hi, w_lo = sem("w_scaled"), sem("w_hi"), sem("w_lo")
        v_mm, q_mm, k_mm, o_mm, f_mm = (sem(n) for n in ("v_mm", "q_mm", "k_mm", "o_mm", "f_mm"))
        score_mm, attn_mm, x1_turned, x2_turned = (
            sem(n) for n in ("score_mm", "attn_mm", "x1_turned", "x2_turned"))
        v_out, q_out, k_out, o_out, f_out, a_out = (
            sem(n) for n in ("v_out", "q_out", "k_out", "o_out", "f_out", "a_out"))
        x1_hi, x1_lo, x2_hi, x2_lo, ctx_hi, ctx_lo, at_hi, at_lo = (
            sem(n) for n in ("x1_hi", "x1_lo", "x2_hi", "x2_lo", "ctx_hi", "ctx_lo", "at_hi", "at_lo"))
        s_turned, s_peak, s_sub, s_exp, s_total, s_inv, s_probs, s_back = (
            sem(n) for n in ("s_turned", "s_peak", "s_sub", "s_exp", "s_total", "s_inv", "s_probs", "s_back"))
        spread_dve, spread_pool = sem("spread_dve"), sem("spread_pool")
        n_stats = [sem(f"n{i}_stats") for i in (1, 2)]
        n_aggr = [sem(f"n{i}_aggr") for i in (1, 2)]
        n_eps = [sem(f"n{i}_eps") for i in (1, 2)]
        n_rstd = [sem(f"n{i}_rstd") for i in (1, 2)]
        n_done = [sem(f"n{i}_done") for i in (1, 2)]
        res_biased, x2_biased = sem("res_biased"), sem("x2_biased")

        x_rows = x.rearrange("b s d -> (b s) d")
        out_rows = out.rearrange("b s d -> (b s) d")

        def tiles_of(rows, c):
            return rows[bass.ds(c * TOK, TOK), :].rearrange("(t p) n -> p t n", p=P)

        def pieces(w):
            return w.rearrange("(k p) n -> p k n", p=P)

        W_ORDER = [("wk", wk_t), ("wq", wq_t), ("wv", wv_t), ("wo", wo_t), ("wf", wf_t)]

        block = stack.enter_context(nc.Block())

        def steps(engine, step, ahead=2):
            step(0)
            step(1)
            with engine.Fori(2, CHUNKS - ahead) as i:
                step(i)
            for i in range(CHUNKS - ahead, CHUNKS + 1):
                step(i)

        def exists(c):
            return not isinstance(c, int) or 0 <= c < CHUNKS

        @block.sync
        def _(sp):
            def load_x(c):
                reached(sp, x1_turned, TILES * c)
                sp.sem_inc(sp_passed, 1)
                sp.dma_start(x_norm[:], tiles_of(x_rows, c)).then_inc(x_in, DMA)

            def load_res(c):
                reached(sp, o_out, TILES * c)
                sp.sem_inc(sp_passed, 1)
                sp.dma_start(x_res[:], tiles_of(x_rows, c)).then_inc(res_in, DMA)

            def load_ctx(c):
                reached(sp, ctx_lo, c)
                sp.sem_inc(sp_passed, 1)
                sp.dma_start(ctx_raw[:], ctx_t[:, bass.ds(c * TOK, TOK)].rearrange(
                    "(k p) n -> p k n", p=P)).then_inc(ctx_in, DMA)

            def move_q(c):
                sp.wait_ge(q_out, KC * (c + 1))
                sp.sem_inc(sp_passed, 1)
                reached(sp, score_mm, 2 * c)
                for t in range(TILES):
                    for q in range(QH):
                        sp.dma_start(
                            q_pad[HD * t:HD * (t + 1), q::QH, t, :],
                            q_t[HD * q:HD * (q + 1), :, P * t:P * (t + 1)]).then_inc(q_moved, DMA)

            def move_k(c):
                sp.wait_ge(k_out, KC * (c + 1))
                sp.sem_inc(sp_passed, 1)
                reached(sp, score_mm, 2 * c)
                for t in range(TILES):
                    for q in range(QH):
                        sp.dma_start(
                            k_keys[HD * t:HD * (t + 1), q::QH, :],
                            k_t[HD * q:HD * (q + 1), :, P * t:P * (t + 1)]).then_inc(k_moved, DMA)

            def save_v(c):
                sp.wait_ge(v_out, TILES * (c + 1))
                sp.sem_inc(sp_passed, 1)
                for t in range(TILES):
                    sp.dma_start(v_scratch[bass.ds(c * TOK + P * t, P), :].rearrange("(n s) e -> s n e", s=2),
                                 v_rows[:, t, :]).then_inc(v_saved, DMA)

            def load_v(c):
                sp.wait_ge(v_saved, TILES * DMA * (c + 1))
                reached(sp, attn_mm, 2 * c)
                sp.sem_inc(sp_passed, 1)
                sp.dma_start(v_keys[:], v_scratch[bass.ds(c * TOK, TOK), :].rearrange(
                    "(o t) (g d) -> (t g) o d", t=OCT, d=HD)).then_inc(v_in, DMA)

            def move_attn(c):
                sp.wait_ge(a_out, 4 * (c + 1))
                sp.sem_inc(sp_passed, 1)
                reached(sp, at_lo, TILES * c)
                for t in range(TILES):
                    for q in range(QH):
                        sp.dma_start(
                            attn_t[HD * q:HD * (q + 1), :, P * t:P * (t + 1)],
                            attn_cols[HD * t:HD * (t + 1), q::QH, :]).then_inc(a_moved[t], DMA)

            def save_y(c):
                for t in range(TILES):
                    sp.wait_ge(f_out, TILES * c + t + 1)
                    sp.sem_inc(sp_passed, 1)
                    sp.dma_start(out_rows[bass.ds(c * TOK + P * t, P), :], x2[:, t, :]).then_inc(y_saved[t], DMA)

            load_x(0)
            load_ctx(0)
            for n, (_, w) in enumerate(W_ORDER):
                if n >= 2:
                    sp.wait_ge(w_lo, n - 1)
                sp.dma_start(w_raw[:, n % 2], pieces(w)).then_inc(w_in[n % 2], DMA)
                if n == 1:
                    for col, dram in ((bq_col, bq), (bk_col, bk)):
                        sp.dma_start(col[:], dram).then_inc(consts_in, DMA)
                    for row, dram in ((bv_row, bv), (bo_row, bo), (bf_row, bf)):
                        sp.dma_start(row[:], dram.partition_broadcast(P)).then_inc(consts_in, DMA)
                    for n_gate, dram in enumerate((g_attn, g_ffn)):
                        sp.dma_start(gates[:, n_gate:n_gate + 1],
                                     dram.partition_broadcast(P)).then_inc(consts_in, DMA)
                    sp.dma_start(x2[:, 0, :], scale.partition_broadcast(P)).then_inc(consts_in, DMA)
                    load_x(1)
                    load_ctx(1)
            sp.wait_ge(zeroed, 2)
            move_k(0)
            move_q(0)
            save_v(0)
            load_v(0)
            load_x(2)

            def sync_step(i):
                if exists(i):
                    load_res(i)
                if exists(i + 2):
                    load_ctx(i + 2)
                if exists(i + 1):
                    move_k(i + 1)
                if exists(i):
                    move_attn(i)
                if exists(i + 1):
                    move_q(i + 1)
                    save_v(i + 1)
                if exists(i - 1):
                    save_y(i - 1)
                if exists(i + 1):
                    load_v(i + 1)
                if exists(i + 3):
                    load_x(i + 3)

            steps(sp, sync_step, ahead=3)
            sp.wait_ge(v_saved, TILES * DMA * CHUNKS)
            for t in range(TILES):
                sp.wait_ge(y_saved[t], DMA * CHUNKS)

        @block.tensor
        def _(pe):
            def bank_free(user, c, b):
                if user in ("v", "o", "f"):
                    pe.wait_ge({"v": v_out, "o": o_out, "f": f_out}[user], TILES * c + b + 1)
                elif user:
                    pe.wait_ge({"q": q_out, "k": k_out}[user], KC * c + 2 * (b + 1))

            def product(dst, left, right):
                terms = [(k, a, b) for k in range(KC) for a, b in ((HI, HI), (HI, LO), (LO, HI))]
                for n, (k, a, b) in enumerate(terms):
                    last = pe.matmul(dst, left(a, k), right(b, k), start=(n == 0), stop=(n == len(terms) - 1))
                return last

            def rows_layer(parts, w, done, ready=None):
                for t in range(TILES):
                    if ready:
                        ready(t)
                    product(acc[t][:], lambda a, k: parts[:, a, k, P * t:P * (t + 1)],
                            lambda b, k: weights[w][:, b, k, :]).then_inc(done, 1)

            def cols_layer(w, parts, done, prev, prev_c):
                for b in range(2):
                    bank_free(prev, prev_c, b)
                    for m in (2 * b, 2 * b + 1):
                        last = product(acc[b][:, TOK * (m % 2):TOK * (m % 2 + 1)],
                                       lambda a, k: weights[w][:, a, k, P * m:P * (m + 1)],
                                       lambda c, k: parts[:, c, k, :])
                    last.then_inc(done, 1)

            def turn(src, done, t):
                for k in range(KC):
                    last = pe.transpose(turn_ps[t][:, P * k:P * (k + 1)], src[:, t, P * k:P * (k + 1)], ident[:])
                last.then_inc(done, 1)

            def turn_x1(c, prev):
                for t in range(TILES):
                    pe.wait_ge(n_done[0], TILES * c + t + 1)
                    prev(t)
                    turn(x_norm, x1_turned, t)

            def turn_x2(c, prev):
                for t in range(TILES):
                    pe.wait_ge(n_done[1], TILES * c + t + 1)
                    prev(t)
                    turn(x2_norm, x2_turned, t)

            def x1_read(c):
                return lambda t: pe.wait_ge(x1_lo, TILES * c + t + 1)

            def x2_read(c):
                return lambda t: pe.wait_ge(x2_lo, TILES * c + t + 1)

            def v_layer(c):
                rows_layer(ctx_parts, "wv", v_mm, lambda t: bank_free("q", c, t))

            def q_layer(c):
                pe.wait_ge(x1_lo, TILES * (c + 1))
                cols_layer("wq", xa_parts, q_mm, "k", c)

            def k_layer(c, prev, prev_c):
                pe.wait_ge(ctx_lo, c + 1)
                cols_layer("wk", ctx_parts, k_mm, prev, prev_c)

            def o_layer(c, prev, prev_c):
                def ready(t):
                    pe.wait_ge(at_lo, TILES * c + t + 1)
                    bank_free(prev, prev_c, t)
                rows_layer(xa_parts, "wo", o_mm, ready)

            def f_layer(c, prev, prev_c):
                def ready(t):
                    pe.wait_ge(x2_lo, TILES * c + t + 1)
                    bank_free(prev, prev_c, t)
                rows_layer(x2_parts, "wf", f_mm, ready)

            def score(c):
                pe.wait_ge(q_moved, DMA * MOVES * (c + 1))
                pe.wait_ge(k_moved, DMA * MOVES * (c + 1))
                for b in range(2):
                    reached(pe, s_turned, 2 * c if isinstance(c, int) and c == 0 else 2 * c - 1 + b)
                    for o in range(OCTS_A_BANK):
                        for pair in range(PAIRS):
                            n = PAIRS * (OCTS_A_BANK * b + o) + pair
                            last = pe.matmul(
                                score_ps[b][HD * pair:HD * (pair + 1), 2 * HT * o:2 * HT * (o + 1)],
                                k_keys[:].rearrange("p g (s n) -> p (g s) n", s=2)[:, :, n],
                                q_pad[:].rearrange("p h t (s n) -> p s (h t) n", s=2)[:, :, :, n],
                                start=True, stop=True)
                    last.then_inc(score_mm, 1)

            def attend(c):
                pe.wait_ge(v_in, DMA * (c + 1))
                pe.wait_ge(spread_dve, c + 1)
                pe.wait_ge(spread_pool, c + 1)
                half = OCTS // 2
                for b in range(2):
                    reached(pe, a_out, 4 * c)
                    for o in range(half // 2):
                        for hf in range(2):
                            for t in range(TILES):
                                octet = half * hf + half // 2 * b + o
                                tile = TILES * hf + t
                                last = pe.matmul(
                                    attn_ps[b][HD * tile:HD * (tile + 1), P * o:P * (o + 1)],
                                    v_keys[:, OCTS * t + octet, :],
                                    spread[:, octet, t::TILES, :], start=True, stop=True)
                    last.then_inc(attn_mm, 1)

            pe.wait_ge(consts_made, 1)
            turn_x1(0, lambda t: None)
            pe.wait_ge(w_lo, 1)
            k_layer(0, None, 0)
            pe.wait_ge(w_lo, 2)
            q_layer(0)
            pe.wait_ge(w_lo, 3)
            v_layer(0)
            turn_x1(1, x1_read(0))

            def tensor_step(i):
                if exists(i):
                    score(i)
                if exists(i - 1):
                    if not exists(i - 2):
                        pe.wait_ge(w_lo, 5)
                    o_layer(i - 1, *(("f", i - 2) if exists(i - 2) else ("v", i)))
                if exists(i + 1):
                    k_layer(i + 1, *(("o", i - 1) if exists(i - 1) else ("v", i)))
                if exists(i):
                    attend(i)
                if exists(i + 1):
                    q_layer(i + 1)
                if exists(i - 1):
                    turn_x2(i - 1, x1_read(i + 1) if exists(i + 1) else x2_read(i - 2))
                if exists(i + 1):
                    v_layer(i + 1)
                if exists(i - 1):
                    f_layer(i - 1, *(("v", i + 1) if exists(i + 1) else ("o", i - 1)))
                if exists(i + 2):
                    turn_x1(i + 2, x2_read(i - 1) if exists(i - 1) else x1_read(i + 1))

            steps(pe, tensor_step)

        @block.scalar
        def _(act):
            def high(dst, src):
                return nc.scalar.activation(dst, src, ACT.Identity)

            def turned_hi(parts, ready, done, c, free):
                for t in range(TILES):
                    act.wait_ge(ready, TILES * c + t + 1)
                    free()
                    high(parts[:, HI, :, P * t:P * (t + 1)],
                         turn_ps[t][:].rearrange("p (k n) -> p k n", k=KC)).then_inc(done, 1)

            def x1_high(c):
                def free():
                    if exists(c - 2):
                        act.wait_ge(o_mm, TILES * (c - 1))
                    else:
                        reached(act, q_mm, 2 * c)
                turned_hi(xa_parts, x1_turned, x1_hi, c, free)

            def x2_high(c):
                turned_hi(x2_parts, x2_turned, x2_hi, c, lambda: reached(act, f_mm, TILES * c))

            def ctx_high(c):
                act.wait_ge(ctx_in, DMA * (c + 1))
                reached(act, v_mm, 2 * c)
                high(ctx_parts[:, HI], ctx_raw[:]).then_inc(ctx_hi, 1)

            def exp(c):
                act.wait_ge(s_sub, c + 1)
                nc.scalar.activation(probs[:], probs[:], ACT.Exp).then_inc(s_exp, 1)

            def cols_bias(c, dst, bias, ready, moved, done):
                reached(act, moved, DMA * MOVES * c)
                for m in range(KC):
                    if m % 2 == 0:
                        act.wait_ge(ready, 2 * c + m // 2 + 1)
                    nc.scalar.activation(dst[:, m, :], acc[m // 2][:, TOK * (m % 2):TOK * (m % 2 + 1)],
                                         ACT.Identity, bias=bias[:, m:m + 1]).then_inc(done, 1)

            def q_bias(c):
                cols_bias(c, q_t, bq_col, q_mm, q_moved, q_out)

            def k_bias(c):
                cols_bias(c, k_t, bk_col, k_mm, k_moved, k_out)

            def attn_copy(c):
                for t in range(TILES):
                    reached(act, a_moved[t], DMA * QH * c)
                for b in range(2):
                    act.wait_ge(attn_mm, 2 * c + b + 1)
                    for hf in range(2):
                        n = P // 4 * hf + P // 8 * b
                        nc.scalar.activation(
                            attn_cols[:].rearrange("p h (s n) -> p (h s) n", s=2)[:, :, n:n + P // 8]
                            .rearrange("p e (o n) -> p o e n", n=PAIRS),
                            attn_ps[b][P // 2 * hf:P // 2 * (hf + 1), :].rearrange(
                                "p (o e n) -> p o e n", e=2 * H, n=PAIRS), ACT.Identity).then_inc(a_out, 1)

            def attn_high(c):
                act.wait_ge(q_mm, 2 * (c + 2) if exists(c + 1) else 2 * CHUNKS)
                for t in range(TILES):
                    act.wait_ge(a_moved[t], DMA * QH * (c + 1))
                    high(xa_parts[:, HI, :, P * t:P * (t + 1)],
                         attn_t[:, :, P * t:P * (t + 1)]).then_inc(at_hi, 1)

            def w_high(n):
                name = W_ORDER[n][0]
                if name == "wf":
                    act.wait_ge(w_scaled, 1)
                else:
                    act.wait_ge(w_in[n % 2], DMA * (n // 2 + 1))
                high(weights[name][:, HI], w_raw[:, n % 2]).then_inc(w_hi, 1)

            w_high(0)
            ctx_high(0)
            x1_high(0)
            w_high(1)
            w_high(2)
            act.wait_ge(consts_in, 8 * DMA)
            nc.scalar.activation(tanh_g[:], gates[:], ACT.Tanh).then_inc(gates_done, 1)
            k_bias(0)
            q_bias(0)
            w_high(3)
            w_high(4)
            ctx_high(1)

            def scalar_step(i):
                if exists(i):
                    exp(i)
                if exists(i + 1):
                    x1_high(i + 1)
                    k_bias(i + 1)
                if exists(i):
                    attn_copy(i)
                if exists(i + 1):
                    q_bias(i + 1)
                if exists(i - 1):
                    x2_high(i - 1)
                if exists(i):
                    attn_high(i)
                if exists(i + 2):
                    ctx_high(i + 2)

            steps(act, scalar_step)

        @block.vector
        def _(dve):
            def low(dst, src, hi):
                return nc.vector.tensor_tensor(dst, src, hi.bitcast(F32), ALU.subtract)

            def turned_lo(parts, hi_done, done, c):
                for t in range(TILES):
                    dve.wait_ge(hi_done, TILES * c + t + 1)
                    n = slice(P * t, P * (t + 1))
                    low(parts[:, LO, :, n], turn_ps[t][:].rearrange("p (k n) -> p k n", k=KC),
                        parts[:, HI, :, n]).then_inc(done, 1)

            def norm_stats(which, src, c):
                for t in range(TILES):
                    if which == 0 and t == 0:
                        dve.wait_ge(x_in, DMA * (c + 1))
                    if which == 1:
                        dve.wait_ge(o_out, TILES * c + t + 1)
                    nc.vector.bn_stats(stats[which][:, t, :], src[:, t, :]).then_inc(n_stats[which], 1)
                dve.wait_ge(n_stats[which], TILES * (c + 1))
                dve.sem_inc(dve_passed, 1)
                for t in range(TILES):
                    nc.vector.bn_aggr(moments[which][:, t, :], stats[which][:, t, :]).then_inc(n_aggr[which], 1)
                dve.wait_ge(n_aggr[which], TILES * (c + 1))
                nc.vector.tensor_scalar(var_eps[which][:], moments[which][:, :, 1], EPS, None,
                                        ALU.add).then_inc(n_eps[which], 1)

            def norm_apply(which, src, dst, c):
                if which == 1:
                    dve.wait_ge(v_saved, TILES * DMA * (c + 2 if exists(c + 1) else CHUNKS))
                dve.wait_ge(n_rstd[which], c + 1)
                for t in range(TILES):
                    nc.vector.tensor_scalar(dst[:, t, :], src[:, t, :], moments[which][:, t, 0:1],
                                            rstd[which][:, t:t + 1], ALU.subtract, ALU.mult
                                            ).then_inc(n_done[which], 1)

            def w_low(n):
                name = W_ORDER[n][0]
                dve.wait_ge(w_hi, n + 1)
                low(weights[name][:, LO], w_raw[:, n % 2], weights[name][:, HI]).then_inc(w_lo, 1)

            def v_bias(c, t):
                dve.wait_ge(v_mm, TILES * c + t + 1)
                if exists(c - 2):
                    dve.wait_ge(x2_turned, TILES * (c - 1))
                else:
                    reached(dve, v_saved, TILES * DMA * c)
                nc.vector.tensor_tensor(v_rows[:, t, :], acc[t][:], bv_row[:], ALU.add).then_inc(v_out, 1)

            def scores_turn(c):
                flat = turned[:].rearrange("p o a g b -> p (o a g b)")
                for b in range(2):
                    dve.wait_ge(score_mm, 2 * c + b + 1)
                    nc.vector.transpose(flat[:, BANK * b:BANK * (b + 1)], score_ps[b][:]).then_inc(s_turned, 1)

            def own(token):
                return turned[:, :, token, :, token]

            def softmax_a(c):
                dve.wait_ge(s_turned, 2 * (c + 1))
                for s in range(2):
                    nc.vector.tensor_reduce(peak[:, :, s], own(s), AXIS_X, ALU.max).then_inc(s_peak, 1)
                for s in range(2):
                    dve.wait_ge(s_peak, 2 * c + s + 1)
                    last = nc.vector.tensor_tensor(probs[:, :, s, :], own(s),
                                                   peak[:, :, s].unsqueeze(2).broadcast_to([P, OCTS, H]),
                                                   ALU.subtract)
                last.then_inc(s_sub, 1)

            def softmax_b(c):
                dve.wait_ge(s_exp, c + 1)
                nc.vector.tensor_reduce(total[:], probs[:], AXIS_X, ALU.add).then_inc(s_total, 1)
                dve.wait_ge(s_total, c + 1)
                nc.vector.reciprocal(inv_total[:], total[:]).then_inc(s_inv, 1)
                dve.wait_ge(s_inv, c + 1)
                nc.vector.tensor_tensor(probs[:], probs[:], inv_total[:].unsqueeze(3).broadcast_to([P, OCTS, 2, H]),
                                        ALU.mult).then_inc(s_probs, 1)
                dve.wait_ge(s_probs, c + 1)
                nc.vector.transpose(probs_t[:].rearrange("p o c -> p (o c)"),
                                    probs[:].rearrange("p o s g -> p (o s g)")).then_inc(s_back, 1)

            def spread_first(c):
                dve.wait_ge(s_back, c + 1)
                reached(dve, attn_mm, 2 * c)
                n = OCTS - POOL_OCTS
                nc.vector.tensor_tensor(
                    spread[:, :n].rearrange("p o h t -> p (o h) t"),
                    probs_t[:, :n].rearrange("p o h -> p (o h)").unsqueeze(2).broadcast_to([P, n * HT, OCT]),
                    same_token[:].unsqueeze(1).broadcast_to([P, n * HT, OCT]), ALU.mult).then_inc(spread_dve, 1)

            def attn_low(c):
                for t in range(TILES):
                    dve.wait_ge(at_hi, TILES * c + t + 1)
                    n = slice(P * t, P * (t + 1))
                    low(xa_parts[:, LO, :, n], attn_t[:, :, n], xa_parts[:, HI, :, n]).then_inc(at_lo, 1)

            def f_residual(c):
                for t in range(TILES):
                    dve.wait_ge(f_mm, TILES * c + t + 1)
                    dve.wait_ge(x2_biased, TILES * c + t + 1)
                    nc.vector.scalar_tensor_tensor(x2[:, t, :], acc[t][:], tanh_g[:, 1:2], x2[:, t, :],
                                                   ALU.mult, ALU.add).then_inc(f_out, 1)

            def o_residual(c, t):
                reached(dve, y_saved[t], DMA * c)
                dve.wait_ge(o_mm, TILES * c + t + 1)
                dve.wait_ge(res_biased, TILES * c + t + 1)
                nc.vector.scalar_tensor_tensor(x2[:, t, :], acc[t][:], tanh_g[:, 0:1], x_res[:, t, :],
                                               ALU.mult, ALU.add).then_inc(o_out, 1)

            nc.vector.memset(k_keys[:], 0.0).then_inc(zeroed, 1)
            norm_stats(0, x_norm, 0)
            nc.vector.memset(q_pad[:], 0.0).then_inc(zeroed, 1)
            norm_apply(0, x_norm, x_norm, 0)
            w_low(0)
            turned_lo(xa_parts, x1_hi, x1_lo, 0)
            w_low(1)
            dve.wait_ge(consts_in, 8 * DMA)
            w_low(2)
            norm_stats(0, x_norm, 1)
            norm_apply(0, x_norm, x_norm, 1)
            dve.wait_ge(w_in[0], 3 * DMA)
            nc.vector.tensor_tensor(w_raw[:, 0], w_raw[:, 0], x2[:, 0, :].unsqueeze(1).broadcast_to([P, KC, D]),
                                    ALU.mult).then_inc(w_scaled, 1)
            dve.wait_ge(gates_done, 1)
            for row, n in ((bo_row, 0), (bf_row, 1)):
                nc.vector.tensor_scalar(row[:], row[:], tanh_g[:, n:n + 1], None, ALU.mult).then_inc(rows_scaled, 1)
            v_bias(0, 0)
            v_bias(0, 1)
            w_low(3)
            w_low(4)

            def vector_step(i):
                if exists(i):
                    scores_turn(i)
                    softmax_a(i)
                if exists(i - 1):
                    o_residual(i - 1, 0)
                if exists(i):
                    softmax_b(i)
                if exists(i - 1):
                    o_residual(i - 1, 1)
                if exists(i):
                    spread_first(i)
                if exists(i + 1):
                    turned_lo(xa_parts, x1_hi, x1_lo, i + 1)
                if exists(i - 1):
                    norm_stats(1, x2, i - 1)
                if exists(i - 1):
                    norm_apply(1, x2, x2_norm, i - 1)
                if exists(i - 1):
                    turned_lo(x2_parts, x2_hi, x2_lo, i - 1)
                if exists(i + 2):
                    norm_stats(0, x_norm, i + 2)
                    norm_apply(0, x_norm, x_norm, i + 2)
                if exists(i + 1):
                    v_bias(i + 1, 0)
                    v_bias(i + 1, 1)
                if exists(i):
                    attn_low(i)
                if exists(i - 1):
                    f_residual(i - 1)

            steps(dve, vector_step)

        @block.gpsimd
        def _(pool):
            def root(which, c):
                pool.wait_ge(n_eps[which], c + 1)
                nc.gpsimd.tensor_tensor(rstd[which][:], var_eps[which][:], minus_half[:],
                                        ALU.pow).then_inc(n_rstd[which], 1)

            def ctx_low(c):
                pool.wait_ge(ctx_hi, c + 1)
                nc.gpsimd.tensor_tensor(ctx_parts[:, LO], ctx_raw[:], ctx_parts[:, HI].bitcast(F32),
                                        ALU.subtract).then_inc(ctx_lo, 1)

            def res_bias(c):
                pool.wait_ge(res_in, DMA * (c + 1))
                for t in range(TILES):
                    nc.gpsimd.tensor_tensor(x_res[:, t, :], x_res[:, t, :], bo_row[:], ALU.add
                                            ).then_inc(res_biased, 1)

            def x2_bias(c):
                for t in range(TILES):
                    pool.wait_ge(n_done[1], TILES * c + t + 1)
                    nc.gpsimd.tensor_tensor(x2[:, t, :], x2[:, t, :], bf_row[:], ALU.add
                                            ).then_inc(x2_biased, 1)

            def spread_last(c):
                pool.wait_ge(s_back, c + 1)
                reached(pool, attn_mm, 2 * c)
                first = OCTS - POOL_OCTS
                nc.gpsimd.tensor_tensor(
                    spread[:, first:].rearrange("p o h t -> p (o h) t"),
                    probs_t[:, first:].rearrange("p o h -> p (o h)").unsqueeze(2).broadcast_to(
                        [P, POOL_OCTS * HT, OCT]),
                    same_token[:].unsqueeze(1).broadcast_to([P, POOL_OCTS * HT, OCT]),
                    ALU.mult).then_inc(spread_pool, 1)

            made = sem("made")
            nc.gpsimd.memset(ident[:], 0.0).then_inc(made, 1)
            nc.gpsimd.memset(same_token[:], 1.0).then_inc(made, 1)
            nc.gpsimd.memset(minus_half[:], -0.5).then_inc(made, 1)
            pool.wait_ge(made, 3)
            nc.gpsimd.affine_select(out=ident[:], in_=ident[:], compare_op=ALU.not_equal, fill=1.0, base=0,
                                    pattern=[[-1, P]], channel_multiplier=1).then_inc(consts_made, 1)
            root(0, 0)
            nc.gpsimd.affine_select(out=same_token[:], in_=same_token[:], compare_op=ALU.is_ge, fill=0.0, base=0,
                                    pattern=[[-H, 2], [-2 * H, PAIRS]], channel_multiplier=1).then_inc(made, 1)
            pool.wait_ge(made, 4)
            nc.gpsimd.affine_select(out=same_token[:], in_=same_token[:], compare_op=ALU.is_ge, fill=0.0,
                                    base=H - 1, pattern=[[H, 2], [2 * H, PAIRS]], channel_multiplier=-1).then_inc(consts_made, 1)
            ctx_low(0)
            root(0, 1)
            ctx_low(1)
            pool.wait_ge(rows_scaled, 2)
            pool.wait_ge(w_lo, 5)
            pool.wait_ge(consts_made, 2)

            def pool_step(i):
                if exists(i):
                    spread_last(i)
                if exists(i - 1):
                    root(1, i - 1)
                    x2_bias(i - 1)
                if exists(i + 2):
                    root(0, i + 2)
                if exists(i):
                    res_bias(i)
                if exists(i + 2):
                    ctx_low(i + 2)

            steps(pool, pool_step)


def kernel(**inputs):
    import numpy as _np
    import concourse.bacc as _bacc
    from concourse import mybir as _mybir
    from concourse.bass_utils import run_bass_kernel_spmd as _run

    a = {k: _np.asarray(v) for k, v in inputs.items()}

    def cols(v):
        return v.reshape(KC, P).T

    arrays = {
        "x": a["x"],
        "ctx_t": a["ctx_2048"].reshape(B * S, D).T,
        "g_attn": a["g_xattn"],
        "g_ffn": a["g_ffn"],
        "wq_t": a["L0_xattn_Wq"].T, "bq": cols(a["L0_xattn_bq"]),
        "wk_t": a["L0_xattn_Wk"].T, "bk": cols(a["L0_xattn_bk"]),
        "wv_t": a["L0_xattn_Wv"].T, "bv": a["L0_xattn_bv"],
        "wo_t": a["L0_xattn_Wo"].T, "bo": a["L0_xattn_bo"],
        "wf_t": a["L0_ffn_weight"].T, "scale": a["L0_ffn_scale_weight"], "bf": a["L0_ffn_bias"],
    }
    arrays = {k: _np.ascontiguousarray(v) for k, v in arrays.items()}
    nc = _bacc.Bacc("TRN2", target_bir_lowering=False, num_devices=1)
    args = [nc.dram_tensor(k, v.shape, _mybir.dt.from_np(v.dtype), kind="ExternalInput").ap()
            for k, v in arrays.items()]
    args.append(nc.dram_tensor("v_scratch", (B * S, D), _mybir.dt.float32, kind="Internal").ap())
    args.append(nc.dram_tensor("out", (B, S, D), _mybir.dt.float32, kind="ExternalOutput").ap())
    gated_attention_kernel(nc, *args)
    r = _run(nc, [arrays], core_ids=[0])
    return r.results[0]["out"]
```

```python
from contextlib import ExitStack

import concourse.bass as bass
from concourse import mybir

F32 = mybir.dt.float32
F32R = mybir.dt.float32r
ALU = mybir.AluOpType
ACT = mybir.ActivationFunctionType
AXIS_X = mybir.AxisListType.X

P = 128
B, S, D = 4, 512, 512
H, HD = 16, 32
KC = D // P
QH = P // HD
TILES = 2
TOK = TILES * P
CHUNKS = B * S // TOK
OCT = 8
OCTS = P // OCT
PAIRS = OCT // 2
HT = H * TILES
BANK = 512
OCTS_A_BANK = BANK // (2 * HT)
POOL_OCTS = 6
LAST_POOL_OCTS = 8
EPS = 1e-5
HI, LO = 0, 1
DMA = 16
MOVES = TILES * QH
IDLE_START, IDLE_SCORES = 12, 6
IDLE_LAST = {CHUNKS - 1: (0, 2), CHUNKS: (4, 3)}


def reached(engine, semaphore, value):
    if not (isinstance(value, int) and value <= 0):
        engine.wait_ge(semaphore, value)


def gated_attention_kernel(nc, x, ctx_t, g_attn, g_ffn, wq_t, bq, wk_t, bk, wv_t, bv, wo_t, bo,
                           wf_t, scale, bf, v_scratch, out):
    stack = ExitStack()
    with stack:
        def sb(name, shape, dt=F32):
            return stack.enter_context(nc.sbuf_tensor(name, shape, dt))

        def psum(name):
            return stack.enter_context(nc.psum_tensor(name, [P, BANK], F32))

        def sem(name):
            return stack.enter_context(nc.semaphore(name))

        weights = {n: sb(f"{n}_parts", [P, 2, KC, D], F32R) for n in ("wv", "wq", "wk", "wo", "wf")}
        ident = sb("ident", [P, P])
        same_token = sb("same_token", [P, OCT])
        bq_col, bk_col = sb("bq_col", [P, KC]), sb("bk_col", [P, KC])
        bv_row, bo_row, bf_row = sb("bv_row", [P, D]), sb("bo_row", [P, D]), sb("bf_row", [P, D])
        scale_row = sb("scale_row", [P, D])
        gates = sb("gates", [P, 2])
        tanh_g = sb("tanh_g", [P, 2])
        minus_half = sb("minus_half", [P, TILES])
        x_norm = sb("x_norm", [P, TILES, D])
        x_res = sb("x_res", [P, TILES, D])
        stats = [sb(f"stats{i}", [P, TILES, 6]) for i in (1, 2)]
        moments = [sb(f"moments{i}", [P, TILES, 2]) for i in (1, 2)]
        var_eps = [sb(f"var_eps{i}", [P, TILES]) for i in (1, 2)]
        rstd = [sb(f"rstd{i}", [P, TILES]) for i in (1, 2)]
        ctx_raw = sb("ctx_raw", [P, KC, TOK])
        ctx_parts = sb("ctx_parts", [P, 2, KC, TOK], F32R)
        xa_parts = sb("xa_parts", [P, 2, KC, TOK], F32R)
        x2_parts = sb("x2_parts", [P, 2, KC, TOK], F32R)
        q_t, k_t = sb("q_t", [P, KC, TOK]), sb("k_t", [P, KC, TOK])
        v_or_norm = sb("v_or_norm", [P, TILES, D])
        v_rows = x2_norm = v_or_norm
        q_pad = sb("q_pad", [P, H, TILES, P])
        k_keys = sb("k_keys", [P, H, P])
        v_keys = sb("v_keys", [P, TILES * OCTS, HD])
        turned = sb("turned", [P, OCTS, 2, H, 2])
        peak = sb("peak", [P, OCTS, 2])
        probs = sb("probs", [P, OCTS, 2, H])
        total = sb("total", [P, OCTS, 2])
        inv_total = sb("inv_total", [P, OCTS, 2])
        probs_t = sb("probs_t", [P, OCTS, HT])
        spread = sb("spread", [P, OCTS, HT, OCT])
        attn_cols = sb("attn_cols", [P // 2, H, P])
        late = sb("late", [P, 2, TOK * KC])
        attn_t = late[:, 0].rearrange("p (k n) -> p k n", k=KC)
        x2 = late[:, 1].rearrange("p (t n) -> p t n", t=TILES)

        spread_flat = spread[:].rearrange("p o h t -> p (o h t)").rearrange("p (s w) -> p s w", s=2)
        w_raw = [w.rearrange("p (k n) -> p k n", k=KC) for w in (
            spread_flat[:, 0], spread_flat[:, 1], late[:].rearrange("p a n -> p (a n)"))]

        acc = [psum(f"acc{i}") for i in range(2)]
        turn_ps = [psum(f"turn_ps{i}") for i in range(2)]
        score_ps = [psum(f"score_ps{i}") for i in range(2)]
        attn_ps = [psum(f"attn_ps{i}") for i in range(2)]

        last_tile = ((acc[1], slice(0, D // 2)), (attn_ps[0], slice(D // 2, D)))

        biases_in, bv_in, consts_in = sem("biases_in"), sem("bv_in"), sem("consts_in")
        x_in, res_in, ctx_in = sem("x_in"), sem("res_in"), sem("ctx_in")
        q_moved, k_moved = sem("q_moved"), sem("k_moved")
        a_moved = [sem(f"a_moved{t}") for t in range(TILES)]
        v_saved, v_in = sem("v_saved"), sem("v_in")
        y_saved = [sem(f"y_saved{t}") for t in range(TILES)]
        sp_passed, dve_passed = sem("sp_passed"), sem("dve_passed")

        zeroed, consts_made, gates_done, rows_scaled = (
            sem("zeroed"), sem("consts_made"), sem("gates_done"), sem("rows_scaled"))
        ctx0_lo = sem("ctx0_lo")
        w_scaled, w_hi, w_lo = sem("w_scaled"), sem("w_hi"), sem("w_lo")
        v_mm, q_mm, k_mm, o_mm, f_mm = (sem(n) for n in ("v_mm", "q_mm", "k_mm", "o_mm", "f_mm"))
        score_mm, attn_mm, x1_turned, x2_turned = (
            sem(n) for n in ("score_mm", "attn_mm", "x1_turned", "x2_turned"))
        v_out, q_out, k_out, o_out, f_out, a_out = (
            sem(n) for n in ("v_out", "q_out", "k_out", "o_out", "f_out", "a_out"))
        x1_hi, x1_lo, x2_hi, x2_lo, ctx_hi, ctx_lo, at_hi, at_lo = (
            sem(n) for n in ("x1_hi", "x1_lo", "x2_hi", "x2_lo", "ctx_hi", "ctx_lo", "at_hi", "at_lo"))
        s_turned, s_peak, s_sub, s_exp, s_total, s_inv, s_probs, s_back = (
            sem(n) for n in ("s_turned", "s_peak", "s_sub", "s_exp", "s_total", "s_inv", "s_probs", "s_back"))
        spread_dve, spread_pool = sem("spread_dve"), sem("spread_pool")
        n_stats = [sem(f"n{i}_stats") for i in (1, 2)]
        n_aggr = [sem(f"n{i}_aggr") for i in (1, 2)]
        n_eps = [sem(f"n{i}_eps") for i in (1, 2)]
        n_rstd = [sem(f"n{i}_rstd") for i in (1, 2)]
        n_done = [sem(f"n{i}_done") for i in (1, 2)]
        res_biased, x2_biased = sem("res_biased"), sem("x2_biased")

        x_rows = x.rearrange("b s d -> (b s) d")
        out_rows = out.rearrange("b s d -> (b s) d")

        def tiles_of(rows, c):
            return rows[bass.ds(c * TOK, TOK), :].rearrange("(t p) n -> p t n", p=P)

        def by_rows(w):
            return w.rearrange("(k p) n -> p k n", p=P)

        W_ORDER = [("wk", wk_t, 0, (0, P, D // 2)), ("wq", wq_t, 1, (0, D // 2)), ("wv", wv_t, 2, (0, D // 2)),
                   ("wo", wo_t, 0, (0, D // 2)), ("wf", wf_t, 2, (0, D // 2))]
        WK, WQ, WV, WO, WF = range(len(W_ORDER))

        def piece(w, n, j):
            starts = (*W_ORDER[n][3], D)
            return w[:, :, starts[j]:starts[j + 1]]

        def pieces_to(n, j):
            return sum(len(W_ORDER[m][3]) for m in range(n)) + j + 1

        w_in = {(n, j): sem(f"{w[0]}_in{j}") for n, w in enumerate(W_ORDER) for j in range(len(w[3]))}

        block = stack.enter_context(nc.Block())

        def steps(engine, step, ahead=2):
            step(0)
            step(1)
            with engine.Fori(2, CHUNKS - ahead) as i:
                step(i)
            for i in range(CHUNKS - ahead, CHUNKS + 1):
                step(i)

        def exists(c):
            return not isinstance(c, int) or 0 <= c < CHUNKS

        def first(c):
            return isinstance(c, int) and c == 0

        def final(c):
            return isinstance(c, int) and c == CHUNKS - 1

        def pool_octs(c):
            return LAST_POOL_OCTS if final(c) else POOL_OCTS

        def late_f(c):
            return isinstance(c, int) and c == CHUNKS - 3

        @block.sync
        def _(sp):
            def load_x(c):
                reached(sp, x1_turned, TILES * c)
                sp.sem_inc(sp_passed, 1)
                sp.dma_start(x_norm[:], tiles_of(x_rows, c)).then_inc(x_in, DMA)

            def load_res(c):
                reached(sp, o_out, TILES * c)
                sp.sem_inc(sp_passed, 1)
                sp.dma_start(x_res[:], tiles_of(x_rows, c)).then_inc(res_in, DMA)

            def load_ctx(c):
                reached(sp, ctx_lo, c)
                if isinstance(c, int) and c == 1:
                    sp.wait_ge(ctx0_lo, 1)
                sp.sem_inc(sp_passed, 1)
                sp.dma_start(ctx_raw[:], ctx_t[:, bass.ds(c * TOK, TOK)].rearrange(
                    "(k p) n -> p k n", p=P)).then_inc(ctx_in, DMA)

            def move_q(c):
                sp.wait_ge(q_out, KC * (c + 1))
                sp.sem_inc(sp_passed, 1)
                reached(sp, score_mm, 2 * c)
                for t in range(TILES):
                    for q in range(QH):
                        sp.dma_start(
                            q_pad[HD * t:HD * (t + 1), q::QH, t, :],
                            q_t[HD * q:HD * (q + 1), :, P * t:P * (t + 1)]).then_inc(q_moved, DMA)

            def move_k(c):
                sp.wait_ge(k_out, KC * (c + 1))
                sp.sem_inc(sp_passed, 1)
                reached(sp, score_mm, 2 * c)
                for t in range(TILES):
                    for q in range(QH):
                        sp.dma_start(
                            k_keys[HD * t:HD * (t + 1), q::QH, :],
                            k_t[HD * q:HD * (q + 1), :, P * t:P * (t + 1)]).then_inc(k_moved, DMA)

            def save_v(c):
                sp.wait_ge(v_out, TILES * (c + 1))
                sp.sem_inc(sp_passed, 1)
                for t in range(TILES):
                    sp.dma_start(v_scratch[bass.ds(c * TOK + P * t, P), :].rearrange("(n s) e -> s n e", s=2),
                                 v_rows[:, t, :]).then_inc(v_saved, DMA)

            def load_v(c):
                sp.wait_ge(v_saved, TILES * DMA * (c + 1))
                reached(sp, attn_mm, 2 * c)
                sp.sem_inc(sp_passed, 1)
                sp.dma_start(v_keys[:], v_scratch[bass.ds(c * TOK, TOK), :].rearrange(
                    "(o t) (g d) -> (t g) o d", t=OCT, d=HD)).then_inc(v_in, DMA)

            def move_attn(c):
                sp.wait_ge(a_out, 4 * (c + 1))
                sp.sem_inc(sp_passed, 1)
                reached(sp, at_lo, TILES * c)
                for t in range(TILES):
                    for q in range(QH):
                        sp.dma_start(
                            attn_t[HD * q:HD * (q + 1), :, P * t:P * (t + 1)],
                            attn_cols[HD * t:HD * (t + 1), q::QH, :]).then_inc(a_moved[t], DMA)

            def save_y(c):
                for t in range(TILES):
                    for n, (_, cols) in enumerate(
                            last_tile if final(c) and t == TILES - 1 else ((None, slice(0, D)),)):
                        sp.wait_ge(f_out, TILES * c + t + n + 1)
                        sp.sem_inc(sp_passed, 1)
                        sp.dma_start(out_rows[bass.ds(c * TOK + P * t, P), cols], x2[:, t, cols]
                                     ).then_inc(y_saved[t], DMA)

            def load_w(n, j):
                _, w, slot, _ = W_ORDER[n]
                for m in range(n):
                    if W_ORDER[m][2] == slot:
                        sp.wait_ge(w_lo, pieces_to(m, len(W_ORDER[m][3]) - 1))
                sp.dma_start(piece(w_raw[slot], n, j), piece(by_rows(w), n, j)).then_inc(w_in[n, j], DMA)

            load_ctx(0)
            load_w(WK, 0)
            load_w(WK, 1)
            load_x(0)
            load_w(WK, 2)
            for col, dram in ((bk_col, bk), (bq_col, bq)):
                sp.dma_start(col[:], dram).then_inc(biases_in, DMA)
            for n in (WQ, WV):
                for j in range(2):
                    load_w(n, j)
            sp.dma_start(bv_row[:], bv.partition_broadcast(P)).then_inc(bv_in, DMA)
            load_x(1)
            load_ctx(1)
            load_w(WO, 0)
            load_w(WO, 1)
            sp.wait_ge(zeroed, 2)
            move_k(0)
            move_q(0)
            save_v(0)
            load_w(WF, 0)
            load_w(WF, 1)
            sp.dma_start(scale_row[:], scale.partition_broadcast(P)).then_inc(consts_in, DMA)
            for n_gate, dram in enumerate((g_attn, g_ffn)):
                sp.dma_start(gates[:, n_gate:n_gate + 1], dram.partition_broadcast(P)).then_inc(consts_in, DMA)
            for row, dram in ((bo_row, bo), (bf_row, bf)):
                sp.dma_start(row[:], dram.partition_broadcast(P)).then_inc(consts_in, DMA)
            load_v(0)
            load_x(2)

            def sync_step(i):
                if late_f(i - 2):
                    save_y(i - 2)
                if exists(i):
                    load_res(i)
                if exists(i + 2):
                    load_ctx(i + 2)
                if exists(i + 1):
                    move_k(i + 1)
                    move_q(i + 1)
                if first(i):
                    sp.wait_ge(w_lo, pieces_to(WF, 1))
                if exists(i):
                    move_attn(i)
                if exists(i + 1):
                    save_v(i + 1)
                if exists(i - 1) and not late_f(i - 1):
                    save_y(i - 1)
                if exists(i + 1):
                    load_v(i + 1)
                if exists(i + 3):
                    load_x(i + 3)

            steps(sp, sync_step, ahead=3)
            sp.wait_ge(v_saved, TILES * DMA * CHUNKS)
            for t in range(TILES):
                sp.wait_ge(y_saved[t], DMA * (CHUNKS + (len(last_tile) - 1 if t == TILES - 1 else 0)))

        @block.tensor
        def _(pe):
            def bank_free(user, c, b):
                if user in ("v", "o", "f"):
                    pe.wait_ge({"v": v_out, "o": o_out, "f": f_out}[user], TILES * c + b + 1)
                elif user:
                    pe.wait_ge({"q": q_out, "k": k_out}[user], KC * c + 2 * (b + 1))

            def product(dst, left, right, low_ready=None):
                terms = [(k, a, b) for a, b in ((HI, HI), (HI, LO), (LO, HI)) for k in range(KC)]
                for n, (k, a, b) in enumerate(terms):
                    if low_ready and (k, a) == (0, LO):
                        low_ready()
                    last = pe.matmul(dst, left(a, k), right(b, k), start=(n == 0), stop=(n == len(terms) - 1))
                return last

            def rows_layer(parts, w, done, high_ready, low_ready=None, halves=False):
                for t in range(TILES):
                    high_ready(t)
                    for n, (bank, cols) in enumerate(
                            last_tile if halves and t == TILES - 1 else ((acc[t], slice(0, D)),)):
                        product(bank[:, cols], lambda a, k: parts[:, a, k, P * t:P * (t + 1)],
                                lambda b, k: weights[w][:, b, k, cols],
                                (lambda: low_ready(t)) if low_ready and n == 0 else None).then_inc(done, 1)

            def cols_layer(w, parts, done, prev, prev_c, w_new=None, between=None):
                for b in range(2):
                    bank_free(prev, prev_c, b)
                    for m in (2 * b, 2 * b + 1):
                        if between and m == 2:
                            between()
                        if w_new is not None and P * m in W_ORDER[w_new][3]:
                            pe.wait_ge(w_lo, pieces_to(w_new, W_ORDER[w_new][3].index(P * m)))
                        last = product(acc[b][:, TOK * (m % 2):TOK * (m % 2 + 1)],
                                       lambda a, k: weights[w][:, a, k, P * m:P * (m + 1)],
                                       lambda c, k: parts[:, c, k, :])
                    last.then_inc(done, 1)

            def turn(src, done, t):
                for k in range(KC):
                    last = pe.transpose(turn_ps[t][:, P * k:P * (k + 1)], src[:, t, P * k:P * (k + 1)], ident[:])
                last.then_inc(done, 1)

            def turn_x1(c, prev):
                for t in range(TILES):
                    pe.wait_ge(n_done[0], TILES * c + t + 1)
                    prev(t)
                    turn(x_norm, x1_turned, t)

            def turn_x2(c, prev, tiles=range(TILES)):
                for t in tiles:
                    pe.wait_ge(n_done[1], TILES * c + t + 1)
                    prev(t)
                    turn(x2_norm, x2_turned, t)

            def x1_read(c):
                return lambda t: pe.wait_ge(x1_lo, TILES * c + t + 1)

            def x2_read(c):
                return lambda t: pe.wait_ge(x2_lo, TILES * c + t + 1)

            def v_layer(c):
                rows_layer(ctx_parts, "wv", v_mm, lambda t: bank_free("q", c, t))

            def q_layer(c, w_new=None):
                pe.wait_ge(x1_lo, TILES * (c + 1))
                cols_layer("wq", xa_parts, q_mm, "k", c, w_new)

            def k_layer(c, prev, prev_c, w_new=None, between=None):
                pe.wait_ge(ctx_lo, c + 1)
                cols_layer("wk", ctx_parts, k_mm, prev, prev_c, w_new, between)

            def o_layer(c, prev, prev_c):
                def high_ready(t):
                    pe.wait_ge(at_hi, TILES * c + t + 1)
                    bank_free(prev, prev_c, t)
                rows_layer(xa_parts, "wo", o_mm, high_ready, lambda t: pe.wait_ge(at_lo, TILES * c + t + 1))

            def f_layer(c, prev, prev_c, in_tile_0=None):
                def high_ready(t):
                    pe.wait_ge(x2_hi, TILES * c + t + 1)
                    bank_free(prev, prev_c, t)

                def low_ready(t):
                    if in_tile_0 and t == 0:
                        in_tile_0()
                    pe.wait_ge(x2_lo, TILES * c + t + 1)
                rows_layer(x2_parts, "wf", f_mm, high_ready, low_ready, halves=final(c))

            def score(c):
                pe.wait_ge(q_moved, DMA * MOVES * (c + 1))
                pe.wait_ge(k_moved, DMA * MOVES * (c + 1))
                for b in range(2):
                    reached(pe, s_turned, 2 * c if isinstance(c, int) and c == 0 else 2 * c - 1 + b)
                    for o in range(OCTS_A_BANK):
                        for pair in range(PAIRS):
                            n = PAIRS * (OCTS_A_BANK * b + o) + pair
                            last = pe.matmul(
                                score_ps[b][HD * pair:HD * (pair + 1), 2 * HT * o:2 * HT * (o + 1)],
                                k_keys[:].rearrange("p g (s n) -> p (g s) n", s=2)[:, :, n],
                                q_pad[:].rearrange("p h t (s n) -> p s (h t) n", s=2)[:, :, :, n],
                                start=True, stop=True)
                    last.then_inc(score_mm, 1)

            def attend(c):
                pe.wait_ge(v_in, DMA * (c + 1))
                pe.wait_ge(spread_dve, c + 1)
                pe.wait_ge(spread_pool, c + 1)
                half = OCTS // 2
                for b in range(2):
                    reached(pe, a_out, 4 * c)
                    for o in range(half // 2):
                        for hf in range(2):
                            for t in range(TILES):
                                octet = half * hf + half // 2 * b + o
                                tile = TILES * hf + t
                                last = pe.matmul(
                                    attn_ps[b][HD * tile:HD * (tile + 1), P * o:P * (o + 1)],
                                    v_keys[:, OCTS * t + octet, :],
                                    spread[:, octet, t::TILES, :], start=True, stop=True)
                    last.then_inc(attn_mm, 1)

            def keep_clock(count):
                for _ in range(count):
                    pe.matmul(score_ps[0][:, :P], ident[:], ident[:], start=True, stop=True)

            pe.wait_ge(consts_made, 1)
            keep_clock(IDLE_START)
            pe.wait_ge(ctx0_lo, 1)
            k_layer(0, None, 0, w_new=WK, between=lambda: turn_x1(0, lambda t: None))
            q_layer(0, w_new=WQ)
            pe.wait_ge(w_lo, pieces_to(WV, 1))
            v_layer(0)
            turn_x1(1, x1_read(0))
            keep_clock(IDLE_SCORES)

            def tensor_step(i):
                if exists(i):
                    score(i)
                if late_f(i - 2):
                    f_layer(i - 2, "v", i)
                if exists(i - 1):
                    if not exists(i - 2):
                        pe.wait_ge(w_lo, pieces_to(WO, 1))
                    o_layer(i - 1, *(("f", i - 2) if exists(i - 2) else ("v", i)))
                if exists(i + 1):
                    k_layer(i + 1, *(("o", i - 1) if exists(i - 1) else ("v", i)))
                    q_layer(i + 1)
                if exists(i):
                    attend(i)
                if exists(i + 1):
                    if exists(i - 1):
                        turn_x2(i - 1, x1_read(i + 1))
                    v_layer(i + 1)
                    if exists(i - 1) and not late_f(i - 1):
                        if not exists(i - 2):
                            pe.wait_ge(w_lo, pieces_to(WF, 1))
                        f_layer(i - 1, "v", i + 1)
                else:
                    keep_clock(IDLE_LAST[i][0])
                    turn_x2(i - 1, x2_read(i - 2), (0,))
                    keep_clock(IDLE_LAST[i][1])
                    f_layer(i - 1, "o", i - 1, lambda: turn_x2(i - 1, x2_read(i - 2), (1,)))
                if exists(i + 2):
                    turn_x1(i + 2, x2_read(i - 1) if exists(i - 1) else x1_read(i + 1))

            steps(pe, tensor_step)

        @block.scalar
        def _(act):
            def high(dst, src):
                return nc.scalar.activation(dst, src, ACT.Identity)

            def turned_hi(parts, ready, done, c, free):
                for t in range(TILES):
                    act.wait_ge(ready, TILES * c + t + 1)
                    free()
                    high(parts[:, HI, :, P * t:P * (t + 1)],
                         turn_ps[t][:].rearrange("p (k n) -> p k n", k=KC)).then_inc(done, 1)

            def x1_high(c):
                def free():
                    if exists(c - 2):
                        act.wait_ge(o_mm, TILES * (c - 1))
                    else:
                        reached(act, q_mm, 2 * c)
                turned_hi(xa_parts, x1_turned, x1_hi, c, free)

            def x2_high(c):
                turned_hi(x2_parts, x2_turned, x2_hi, c, lambda: reached(act, f_mm, TILES * c))

            def ctx_high(c):
                act.wait_ge(ctx_in, DMA * (c + 1))
                reached(act, v_mm, 2 * c)
                high(ctx_parts[:, HI], ctx_raw[:]).then_inc(ctx_hi, 1)

            def exp(c):
                act.wait_ge(s_sub, c + 1)
                nc.scalar.activation(probs[:], probs[:], ACT.Exp).then_inc(s_exp, 1)

            def cols_bias(c, dst, bias, ready, moved, done):
                reached(act, moved, DMA * MOVES * c)
                for m in range(KC):
                    if m % 2 == 0:
                        act.wait_ge(ready, 2 * c + m // 2 + 1)
                    nc.scalar.activation(dst[:, m, :], acc[m // 2][:, TOK * (m % 2):TOK * (m % 2 + 1)],
                                         ACT.Identity, bias=bias[:, m:m + 1]).then_inc(done, 1)

            def q_bias(c):
                cols_bias(c, q_t, bq_col, q_mm, q_moved, q_out)

            def k_bias(c):
                cols_bias(c, k_t, bk_col, k_mm, k_moved, k_out)

            def attn_copy(c):
                for t in range(TILES):
                    reached(act, a_moved[t], DMA * QH * c)
                for b in range(2):
                    act.wait_ge(attn_mm, 2 * c + b + 1)
                    for hf in range(2):
                        n = P // 4 * hf + P // 8 * b
                        nc.scalar.activation(
                            attn_cols[:].rearrange("p h (s n) -> p (h s) n", s=2)[:, :, n:n + P // 8]
                            .rearrange("p e (o n) -> p o e n", n=PAIRS),
                            attn_ps[b][P // 2 * hf:P // 2 * (hf + 1), :].rearrange(
                                "p (o e n) -> p o e n", e=2 * H, n=PAIRS), ACT.Identity).then_inc(a_out, 1)

            def attn_high(c):
                act.wait_ge(q_mm, 2 * (c + 2) if exists(c + 1) else 2 * CHUNKS)
                for t in range(TILES):
                    act.wait_ge(a_moved[t], DMA * QH * (c + 1))
                    high(xa_parts[:, HI, :, P * t:P * (t + 1)],
                         attn_t[:, :, P * t:P * (t + 1)]).then_inc(at_hi, 1)

            def w_high(n, j):
                name, _, slot, _ = W_ORDER[n]
                if n == WF:
                    act.wait_ge(w_scaled, j + 1)
                else:
                    act.wait_ge(w_in[n, j], DMA)
                high(piece(weights[name][:, HI], n, j), piece(w_raw[slot], n, j)).then_inc(w_hi, 1)

            ctx_high(0)
            for n, j in ((WK, 0), (WK, 1), (WK, 2), (WQ, 0), (WQ, 1)):
                w_high(n, j)
            x1_high(0)
            act.wait_ge(biases_in, 2 * DMA)
            k_bias(0)
            w_high(WV, 0)
            w_high(WV, 1)
            q_bias(0)
            w_high(WO, 0)
            w_high(WO, 1)
            ctx_high(1)
            x1_high(1)

            def scalar_step(i):
                if exists(i):
                    exp(i)
                if exists(i + 1):
                    if not first(i):
                        x1_high(i + 1)
                    k_bias(i + 1)
                if first(i):
                    act.wait_ge(consts_in, 5 * DMA)
                    nc.scalar.activation(tanh_g[:], gates[:], ACT.Tanh).then_inc(gates_done, 1)
                if exists(i + 1):
                    q_bias(i + 1)
                if first(i):
                    w_high(WF, 0)
                    w_high(WF, 1)
                if exists(i):
                    attn_copy(i)
                if exists(i - 1):
                    x2_high(i - 1)
                if exists(i):
                    attn_high(i)
                if exists(i + 2):
                    ctx_high(i + 2)

            steps(act, scalar_step)

        @block.vector
        def _(dve):
            def low(dst, src, hi):
                return nc.vector.tensor_tensor(dst, src, hi.bitcast(F32), ALU.subtract)

            def turned_lo(parts, hi_done, done, c, tiles=range(TILES)):
                for t in tiles:
                    dve.wait_ge(hi_done, TILES * c + t + 1)
                    n = slice(P * t, P * (t + 1))
                    low(parts[:, LO, :, n], turn_ps[t][:].rearrange("p (k n) -> p k n", k=KC),
                        parts[:, HI, :, n]).then_inc(done, 1)

            def row_stats(which, src, c, t):
                if which == 0 and t == 0:
                    dve.wait_ge(x_in, DMA * (c + 1))
                if which == 1:
                    dve.wait_ge(o_out, TILES * c + t + 1)
                nc.vector.bn_stats(stats[which][:, t, :], src[:, t, :]).then_inc(n_stats[which], 1)

            def variance(which, c, tiles):
                done = TILES * c + tiles[-1] + 1
                dve.wait_ge(n_stats[which], done)
                dve.sem_inc(dve_passed, 1)
                for t in tiles:
                    nc.vector.bn_aggr(moments[which][:, t, :], stats[which][:, t, :]).then_inc(n_aggr[which], 1)
                dve.wait_ge(n_aggr[which], done)
                t = slice(tiles[0], tiles[-1] + 1)
                nc.vector.tensor_scalar(var_eps[which][:, t], moments[which][:, t, 1], EPS, None,
                                        ALU.add).then_inc(n_eps[which], len(tiles))

            def norm_stats(which, src, c, tiles=(0, 1)):
                for t in tiles:
                    row_stats(which, src, c, t)
                variance(which, c, tiles)

            def norm_apply(which, src, dst, c, tiles=(0, 1)):
                dve.wait_ge(n_rstd[which], TILES * c + tiles[-1] + 1)
                for t in tiles:
                    nc.vector.tensor_scalar(dst[:, t, :], src[:, t, :], moments[which][:, t, 0:1],
                                            rstd[which][:, t:t + 1], ALU.subtract, ALU.mult
                                            ).then_inc(n_done[which], 1)

            def second_stats(c, t):
                norm_stats(1, x2, c, (t,))

            def second_apply(c, t):
                if t == 0:
                    dve.wait_ge(v_saved, TILES * DMA * (c + 2 if exists(c + 1) else CHUNKS))
                norm_apply(1, x2, x2_norm, c, (t,))

            def scale_w(j):
                dve.wait_ge(w_in[WF, j], DMA)
                raw = piece(w_raw[W_ORDER[WF][2]], WF, j)
                nc.vector.tensor_tensor(raw, raw, scale_row[:, D // 2 * j:D // 2 * (j + 1)].unsqueeze(1)
                                        .broadcast_to([P, KC, D // 2]), ALU.mult).then_inc(w_scaled, 1)

            def w_low(n, j):
                name, _, slot, _ = W_ORDER[n]
                dve.wait_ge(w_hi, pieces_to(n, j))
                low(piece(weights[name][:, LO], n, j), piece(w_raw[slot], n, j),
                    piece(weights[name][:, HI], n, j)).then_inc(w_lo, 1)

            def v_bias(c, t):
                dve.wait_ge(v_mm, TILES * c + t + 1)
                if exists(c - 2):
                    dve.wait_ge(x2_turned, TILES * (c - 1))
                else:
                    reached(dve, v_saved, TILES * DMA * c)
                nc.vector.tensor_tensor(v_rows[:, t, :], acc[t][:], bv_row[:], ALU.add).then_inc(v_out, 1)

            def scores_turn(c):
                flat = turned[:].rearrange("p o a g b -> p (o a g b)")
                for b in range(2):
                    dve.wait_ge(score_mm, 2 * c + b + 1)
                    nc.vector.transpose(flat[:, BANK * b:BANK * (b + 1)], score_ps[b][:]).then_inc(s_turned, 1)

            def own(token):
                return turned[:, :, token, :, token]

            def softmax_a(c):
                dve.wait_ge(s_turned, 2 * (c + 1))
                for s in range(2):
                    nc.vector.tensor_reduce(peak[:, :, s], own(s), AXIS_X, ALU.max).then_inc(s_peak, 1)
                for s in range(2):
                    dve.wait_ge(s_peak, 2 * c + s + 1)
                    last = nc.vector.tensor_tensor(probs[:, :, s, :], own(s),
                                                   peak[:, :, s].unsqueeze(2).broadcast_to([P, OCTS, H]),
                                                   ALU.subtract)
                last.then_inc(s_sub, 1)

            def softmax_b(c):
                dve.wait_ge(s_exp, c + 1)
                nc.vector.tensor_reduce(total[:], probs[:], AXIS_X, ALU.add).then_inc(s_total, 1)
                dve.wait_ge(s_total, c + 1)
                nc.vector.reciprocal(inv_total[:], total[:]).then_inc(s_inv, 1)
                dve.wait_ge(s_inv, c + 1)
                nc.vector.tensor_tensor(probs[:], probs[:], inv_total[:].unsqueeze(3).broadcast_to([P, OCTS, 2, H]),
                                        ALU.mult).then_inc(s_probs, 1)
                dve.wait_ge(s_probs, c + 1)
                nc.vector.transpose(probs_t[:].rearrange("p o c -> p (o c)"),
                                    probs[:].rearrange("p o s g -> p (o s g)")).then_inc(s_back, 1)

            def spread_first(c):
                dve.wait_ge(s_back, c + 1)
                reached(dve, attn_mm, 2 * c)
                n = OCTS - pool_octs(c)
                nc.vector.tensor_tensor(
                    spread[:, :n].rearrange("p o h t -> p (o h) t"),
                    probs_t[:, :n].rearrange("p o h -> p (o h)").unsqueeze(2).broadcast_to([P, n * HT, OCT]),
                    same_token[:].unsqueeze(1).broadcast_to([P, n * HT, OCT]), ALU.mult).then_inc(spread_dve, 1)

            def attn_low(c, t):
                dve.wait_ge(at_hi, TILES * c + t + 1)
                n = slice(P * t, P * (t + 1))
                low(xa_parts[:, LO, :, n], attn_t[:, :, n], xa_parts[:, HI, :, n]).then_inc(at_lo, 1)

            def f_residual(c, t):
                dve.wait_ge(x2_biased, TILES * c + t + 1)
                for n, (bank, cols) in enumerate(
                        last_tile if final(c) and t == TILES - 1 else ((acc[t], slice(0, D)),)):
                    dve.wait_ge(f_mm, TILES * c + t + n + 1)
                    nc.vector.scalar_tensor_tensor(x2[:, t, cols], bank[:, cols], tanh_g[:, 1:2], x2[:, t, cols],
                                                   ALU.mult, ALU.add).then_inc(f_out, 1)

            def o_residual(c, t):
                reached(dve, y_saved[t], DMA * c)
                dve.wait_ge(o_mm, TILES * c + t + 1)
                dve.wait_ge(res_biased, TILES * c + t + 1)
                nc.vector.scalar_tensor_tensor(x2[:, t, :], acc[t][:], tanh_g[:, 0:1], x_res[:, t, :],
                                               ALU.mult, ALU.add).then_inc(o_out, 1)

            nc.vector.memset(k_keys[:], 0.0).then_inc(zeroed, 1)
            dve.wait_ge(ctx_hi, 1)
            low(ctx_parts[:, LO, :KC // 2], ctx_raw[:, :KC // 2], ctx_parts[:, HI, :KC // 2]).then_inc(ctx0_lo, 1)
            w_low(WK, 0)
            w_low(WK, 1)
            norm_stats(0, x_norm, 0)
            norm_apply(0, x_norm, x_norm, 0)
            w_low(WK, 2)
            w_low(WQ, 0)
            turned_lo(xa_parts, x1_hi, x1_lo, 0)
            w_low(WQ, 1)
            w_low(WV, 0)
            w_low(WV, 1)
            norm_stats(0, x_norm, 1)
            norm_apply(0, x_norm, x_norm, 1)
            dve.wait_ge(bv_in, DMA)
            v_bias(0, 0)
            w_low(WO, 0)
            w_low(WO, 1)
            v_bias(0, 1)
            turned_lo(xa_parts, x1_hi, x1_lo, 1)

            def vector_step(i):
                if final(i - 1):
                    return last_step(i)
                scores_turn(i)
                if first(i - 1):
                    o_residual(i - 1, 0)
                softmax_a(i)
                if final(i):
                    return last_softmax_step(i)
                if first(i - 1):
                    o_residual(i - 1, 1)
                elif exists(i - 1):
                    o_residual(i - 1, 0)
                softmax_b(i)
                if exists(i - 1) and not first(i - 1):
                    o_residual(i - 1, 1)
                if exists(i + 1) and not first(i):
                    turned_lo(xa_parts, x1_hi, x1_lo, i + 1)
                spread_first(i)
                if first(i):
                    dve.wait_ge(consts_in, 5 * DMA)
                    scale_w(0)
                    scale_w(1)
                    dve.wait_ge(gates_done, 1)
                    for row, n in ((bo_row, 0), (bf_row, 1)):
                        nc.vector.tensor_scalar(row[:], row[:], tanh_g[:, n:n + 1], None,
                                                ALU.mult).then_inc(rows_scaled, 1)
                if exists(i - 1):
                    for t in range(TILES):
                        second_stats(i - 1, t)
                        second_apply(i - 1, t)
                if exists(i + 2):
                    norm_stats(0, x_norm, i + 2)
                    if first(i):
                        w_low(WF, 0)
                        w_low(WF, 1)
                    norm_apply(0, x_norm, x_norm, i + 2)
                if exists(i - 1):
                    turned_lo(x2_parts, x2_hi, x2_lo, i - 1)
                v_bias(i + 1, 0)
                v_bias(i + 1, 1)
                if not late_f(i - 1):
                    attn_low(i, 0)
                    attn_low(i, 1)
                    if exists(i - 1):
                        f_residual(i - 1, 0)
                        f_residual(i - 1, 1)

            def last_softmax_step(i):
                attn_low(i - 1, 0)
                attn_low(i - 1, 1)
                f_residual(i - 2, 0)
                softmax_b(i)
                f_residual(i - 2, 1)
                spread_first(i)
                o_residual(i - 1, 0)
                second_stats(i - 1, 0)
                o_residual(i - 1, 1)
                second_apply(i - 1, 0)
                second_stats(i - 1, 1)
                turned_lo(x2_parts, x2_hi, x2_lo, i - 1, (0,))
                second_apply(i - 1, 1)
                turned_lo(x2_parts, x2_hi, x2_lo, i - 1, (1,))
                for t in range(TILES):
                    f_residual(i - 1, t)
                    attn_low(i, t)

            def last_step(i):
                o_residual(i - 1, 0)
                second_stats(i - 1, 0)
                second_apply(i - 1, 0)
                o_residual(i - 1, 1)
                second_stats(i - 1, 1)
                turned_lo(x2_parts, x2_hi, x2_lo, i - 1, (0,))
                second_apply(i - 1, 1)
                turned_lo(x2_parts, x2_hi, x2_lo, i - 1, (1,))
                f_residual(i - 1, 0)
                f_residual(i - 1, 1)

            steps(dve, vector_step)

        @block.gpsimd
        def _(pool):
            def root(which, c, first=0, count=TILES):
                t = slice(first, first + count)
                pool.wait_ge(n_eps[which], TILES * c + first + count)
                nc.gpsimd.tensor_tensor(rstd[which][:, t], var_eps[which][:, t], minus_half[:, t],
                                        ALU.pow).then_inc(n_rstd[which], count)

            def ctx_low(c, first_k=0):
                pool.wait_ge(ctx_hi, c + 1)
                k = slice(first_k, KC)
                nc.gpsimd.tensor_tensor(ctx_parts[:, LO, k], ctx_raw[:, k], ctx_parts[:, HI, k].bitcast(F32),
                                        ALU.subtract).then_inc(ctx_lo, 1)

            def res_bias(c):
                pool.wait_ge(res_in, DMA * (c + 1))
                for t in range(TILES):
                    nc.gpsimd.tensor_tensor(x_res[:, t, :], x_res[:, t, :], bo_row[:], ALU.add
                                            ).then_inc(res_biased, 1)

            def x2_bias(c):
                for t in range(TILES):
                    pool.wait_ge(n_done[1], TILES * c + t + 1)
                    nc.gpsimd.tensor_tensor(x2[:, t, :], x2[:, t, :], bf_row[:], ALU.add
                                            ).then_inc(x2_biased, 1)

            def spread_last(c):
                pool.wait_ge(s_back, c + 1)
                reached(pool, attn_mm, 2 * c)
                first = OCTS - pool_octs(c)
                nc.gpsimd.tensor_tensor(
                    spread[:, first:].rearrange("p o h t -> p (o h) t"),
                    probs_t[:, first:].rearrange("p o h -> p (o h)").unsqueeze(2).broadcast_to(
                        [P, pool_octs(c) * HT, OCT]),
                    same_token[:].unsqueeze(1).broadcast_to([P, pool_octs(c) * HT, OCT]),
                    ALU.mult).then_inc(spread_pool, 1)

            made = sem("made")
            nc.gpsimd.memset(ident[:], 0.0).then_inc(made, 1)
            nc.gpsimd.memset(same_token[:], 1.0).then_inc(made, 1)
            nc.gpsimd.memset(minus_half[:], -0.5).then_inc(made, 1)
            pool.wait_ge(made, 3)
            nc.gpsimd.affine_select(out=ident[:], in_=ident[:], compare_op=ALU.not_equal, fill=1.0, base=0,
                                    pattern=[[-1, P]], channel_multiplier=1).then_inc(consts_made, 1)
            nc.gpsimd.affine_select(out=same_token[:], in_=same_token[:], compare_op=ALU.is_ge, fill=0.0, base=0,
                                    pattern=[[-H, 2], [-2 * H, PAIRS]], channel_multiplier=1).then_inc(made, 1)
            pool.wait_ge(made, 4)
            nc.gpsimd.affine_select(out=same_token[:], in_=same_token[:], compare_op=ALU.is_ge, fill=0.0,
                                    base=H - 1, pattern=[[H, 2], [2 * H, PAIRS]], channel_multiplier=-1).then_inc(consts_made, 1)
            ctx_low(0, KC // 2)
            root(0, 0)
            nc.gpsimd.memset(q_pad[:], 0.0).then_inc(zeroed, 1)
            root(0, 1)
            ctx_low(1)
            pool.wait_ge(w_lo, pieces_to(WO, 1))
            pool.wait_ge(consts_made, 2)

            def pool_step(i):
                if exists(i):
                    spread_last(i)
                if exists(i - 1):
                    root(1, i - 1, 0, 1)
                    root(1, i - 1, 1, 1)
                if exists(i + 2):
                    root(0, i + 2)
                if exists(i - 1):
                    x2_bias(i - 1)
                if exists(i):
                    if first(i):
                        pool.wait_ge(rows_scaled, 2)
                    res_bias(i)
                if exists(i + 2):
                    ctx_low(i + 2)

            steps(pool, pool_step)


def kernel(**inputs):
    import numpy as _np
    import concourse.bacc as _bacc
    from concourse import mybir as _mybir
    from concourse.bass_utils import run_bass_kernel_spmd as _run

    a = {k: _np.asarray(v) for k, v in inputs.items()}

    def cols(v):
        return v.reshape(KC, P).T

    arrays = {
        "x": a["x"],
        "ctx_t": a["ctx_2048"].reshape(B * S, D).T,
        "g_attn": a["g_xattn"],
        "g_ffn": a["g_ffn"],
        "wq_t": a["L0_xattn_Wq"].T, "bq": cols(a["L0_xattn_bq"]),
        "wk_t": a["L0_xattn_Wk"].T, "bk": cols(a["L0_xattn_bk"]),
        "wv_t": a["L0_xattn_Wv"].T, "bv": a["L0_xattn_bv"],
        "wo_t": a["L0_xattn_Wo"].T, "bo": a["L0_xattn_bo"],
        "wf_t": a["L0_ffn_weight"].T, "scale": a["L0_ffn_scale_weight"], "bf": a["L0_ffn_bias"],
    }
    arrays = {k: _np.ascontiguousarray(v) for k, v in arrays.items()}
    nc = _bacc.Bacc("TRN2", target_bir_lowering=False, num_devices=1)
    args = [nc.dram_tensor(k, v.shape, _mybir.dt.from_np(v.dtype), kind="ExternalInput").ap()
            for k, v in arrays.items()]
    args.append(nc.dram_tensor("v_scratch", (B * S, D), _mybir.dt.float32, kind="Internal").ap())
    args.append(nc.dram_tensor("out", (B, S, D), _mybir.dt.float32, kind="ExternalOutput").ap())
    gated_attention_kernel(nc, *args)
    r = _run(nc, [arrays], core_ids=[0])
    return r.results[0]["out"]
```
